# Optimizing a Trainium2 kernel written in Bass

```python
import numpy as np
import jax
import jax.numpy as jnp

def _softmax(x, axis=-1):
    return jax.nn.softmax(x, axis=axis)

def _gelu(x):
    return jax.nn.gelu(x, approximate=True)

def _silu(x):
    return jax.nn.silu(x)

def _sigmoid(x):
    return jax.nn.sigmoid(x)

def _layernorm(x, axis=-1, eps=1e-05):
    m = jnp.mean(x, axis=axis, keepdims=True)
    v = jnp.var(x, axis=axis, keepdims=True)
    return (x - m) / jnp.sqrt(v + eps)

def _scatter_add(tgt, idx, src, axis=0):
    return tgt.at[idx].add(src)

def _segment_sum(src, seg, n):
    return jax.ops.segment_sum(src, seg, n)
kernel_name = 'mk_lm_tower_d1_tok_ids2048_r4_246ce0'

def setup_inputs(seed: int=0):
    np.random.seed(seed)
    _w = jnp.asarray

    def _rec_inputs():
        import jax
        import jax.numpy as jnp
        _rk = jax.random.key(seed)
        x = jax.random.randint(jax.random.fold_in(_rk, 1), (1, 2048), 0, 128, jnp.int32)
        return x
    x = _rec_inputs()

    def _L0_tok_setup():
        import jax, jax.numpy as jnp
        import numpy as np
        VOCAB = 128
        D_VIS = 512
        D_TXT = 512
        EPS = 1e-06
        VOCAB_OFFSET = 0

        def rms_norm(x, weight, eps):
            xf = x.astype(jnp.float32)
            var = jnp.mean(xf * xf, axis=-1, keepdims=True)
            normed = xf * jax.lax.rsqrt(var + eps)
            if weight is not None:
                normed = normed * weight.astype(jnp.float32)
            return normed.astype(x.dtype)
        key = jax.random.key(seed)
        k_ids, k_emb, k_w, k_proj = jax.random.split(key, 4)
        input_ids = jax.random.randint(k_ids, (8, 1024), 0, VOCAB, dtype=jnp.int64)
        emb_table = jax.random.normal(k_emb, (VOCAB, D_VIS), dtype=jnp.float32) * 0.02
        norm_weight = jnp.ones((D_VIS,), dtype=jnp.float32) + 0.01 * jax.random.normal(k_w, (D_VIS,), dtype=jnp.float32)
        proj_weight = jax.random.normal(k_proj, (D_TXT, D_VIS), dtype=jnp.float32) * 0.02
        return {'input_ids': input_ids, 'emb_table': emb_table, 'norm_weight': norm_weight, 'proj_weight': proj_weight}
    _L0_tok_all = _L0_tok_setup()
    _L0_tok_in = {k: v for k, v in _L0_tok_all.items() if k in ('emb_table', 'norm_weight', 'proj_weight')}
    del _L0_tok_all

    def _L0_attn_setup():
        import jax, jax.numpy as jnp
        import numpy as np
        B, S, H = (4, 512, 512)
        key = jax.random.key(seed)
        k1, k2, k3 = jax.random.split(key, 3)
        xav_qkv = float(np.sqrt(6.0 / (H + 3 * H)))
        xav_out = float(np.sqrt(6.0 / (H + H)))
        return {'hidden_states': jax.random.normal(k1, (B, S, H), dtype=jnp.float32), 'w_qkv': jax.random.uniform(k2, (3 * H, H), minval=-xav_qkv, maxval=xav_qkv, dtype=jnp.float32), 'b_qkv': jnp.zeros((3 * H,), dtype=jnp.float32), 'w_out': jax.random.uniform(k3, (H, H), minval=-xav_out, maxval=xav_out, dtype=jnp.float32), 'b_out': jnp.zeros((H,), dtype=jnp.float32)}
    _L0_attn_all = _L0_attn_setup()
    _L0_attn_in = {k: v for k, v in _L0_attn_all.items() if k in ('w_qkv', 'b_qkv', 'w_out', 'b_out')}
    del _L0_attn_all

    def _L0_ffn_setup():
        import jax, jax.numpy as jnp
        import numpy as np
        NUM_EXPERTS = 8
        TOP_K = 2
        HIDDEN = 512
        INTER = 704
        BSZ, SEQ = (4, 512)
        key = jax.random.key(seed)
        ks = jax.random.split(key, 6)
        s = 0.02
        return {'hidden_states': jax.random.normal(ks[0], (BSZ, SEQ, HIDDEN), jnp.float32), 'gate_w': jax.random.normal(ks[1], (NUM_EXPERTS, HIDDEN), jnp.float32) * s, 'gate_b': jnp.zeros((NUM_EXPERTS,), jnp.float32), 'expert_bias': jax.random.normal(ks[2], (NUM_EXPERTS,), jnp.float32) * 0.01, 'w_gate_up': jax.random.normal(ks[3], (NUM_EXPERTS, 2 * INTER, HIDDEN), jnp.float32) * s, 'w_down': jax.random.normal(ks[4], (NUM_EXPERTS, HIDDEN, INTER), jnp.float32) * s}
    _L0_ffn_all = _L0_ffn_setup()
    _L0_ffn_in = {k: v for k, v in _L0_ffn_all.items() if k in ('gate_w', 'gate_b', 'expert_bias', 'w_gate_up', 'w_down')}
    del _L0_ffn_all
    return {'x': x, 'L0_tok_emb_table': _L0_tok_in['emb_table'], 'L0_tok_norm_weight': _L0_tok_in['norm_weight'], 'L0_tok_proj_weight': _L0_tok_in['proj_weight'], 'L0_attn_w_qkv': _L0_attn_in['w_qkv'], 'L0_attn_b_qkv': _L0_attn_in['b_qkv'], 'L0_attn_w_out': _L0_attn_in['w_out'], 'L0_attn_b_out': _L0_attn_in['b_out'], 'L0_ffn_gate_w': _L0_ffn_in['gate_w'], 'L0_ffn_gate_b': _L0_ffn_in['gate_b'], 'L0_ffn_expert_bias': _L0_ffn_in['expert_bias'], 'L0_ffn_w_gate_up': _L0_ffn_in['w_gate_up'], 'L0_ffn_w_down': _L0_ffn_in['w_down']}

def reference(x, L0_tok_emb_table, L0_tok_norm_weight, L0_tok_proj_weight, L0_attn_w_qkv, L0_attn_b_qkv, L0_attn_w_out, L0_attn_b_out, L0_ffn_gate_w, L0_ffn_gate_b, L0_ffn_expert_bias, L0_ffn_w_gate_up, L0_ffn_w_down):
    import jax
    import jax.numpy as jnp

    def _L0_tok_ref(input_ids, emb_table, norm_weight, proj_weight):
        import jax, jax.numpy as jnp
        import numpy as np
        VOCAB = 128
        D_VIS = 512
        D_TXT = 512
        EPS = 1e-06
        VOCAB_OFFSET = 0

        def rms_norm(x, weight, eps):
            xf = x.astype(jnp.float32)
            var = jnp.mean(xf * xf, axis=-1, keepdims=True)
            normed = xf * jax.lax.rsqrt(var + eps)
            if weight is not None:
                normed = normed * weight.astype(jnp.float32)
            return normed.astype(x.dtype)
        hard_emb = emb_table[input_ids - VOCAB_OFFSET]
        hard_emb_norm = rms_norm(hard_emb, norm_weight, EPS)
        proj = jnp.einsum('bsd,ed->bse', hard_emb_norm, proj_weight)
        return rms_norm(proj, None, EPS)

    def _L0_attn_ref(hidden_states, w_qkv, b_qkv, w_out, b_out):
        import jax, jax.numpy as jnp
        import numpy as np
        B, S, H = (4, 512, 512)
        Bc, Sc, Hc = hidden_states.shape
        scaling = jnp.sqrt(jnp.asarray(Hc, hidden_states.dtype))
        qkv = jnp.einsum('bsh,oh->bso', hidden_states, w_qkv) + b_qkv
        q, k, v = jnp.split(qkv, 3, axis=-1)
        scores = jnp.einsum('bqh,bkh->bqk', q, k) / scaling
        probs = jax.nn.softmax(scores, axis=-1)
        context = jnp.einsum('bqk,bkh->bqh', probs, v)
        out = jnp.einsum('bsh,oh->bso', context, w_out) + b_out
        return out

    def _L0_ffn_ref(hidden_states, gate_w, gate_b, expert_bias, w_gate_up, w_down):
        import jax, jax.numpy as jnp
        import numpy as np
        NUM_EXPERTS = 8
        TOP_K = 2
        HIDDEN = 512
        INTER = 704
        BSZ, SEQ = (4, 512)
        bsz, seq_len, hidden_dim = hidden_states.shape
        x = hidden_states.reshape(-1, hidden_dim)
        T = x.shape[0]
        E = w_gate_up.shape[0]
        router_logits = x @ gate_w.T + gate_b
        routing = jax.nn.softmax(router_logits.astype(jnp.float32), axis=-1)
        routing = routing + expert_bias.astype(jnp.float32)
        topk_w, topk_idx = jax.lax.top_k(routing, TOP_K)
        topk_w = topk_w.astype(x.dtype)
        comb = jnp.zeros((T, E), x.dtype).at[jnp.arange(T)[:, None], topk_idx].add(topk_w)
        out = jnp.zeros_like(x)
        for e in range(E):
            gate_up = x @ w_gate_up[e].T
            g, u = jnp.split(gate_up, 2, axis=1)
            inter = jax.nn.silu(g) * u
            out = out + inter @ w_down[e].T * comb[:, e:e + 1]
        return out.reshape(bsz, seq_len, hidden_dim)
    h = _L0_tok_ref(x, L0_tok_emb_table, L0_tok_norm_weight, L0_tok_proj_weight)
    h = h + _L0_attn_ref(_layernorm(h, axis=-1), L0_attn_w_qkv, L0_attn_b_qkv, L0_attn_w_out, L0_attn_b_out)
    h = h + _L0_ffn_ref(_layernorm(h, axis=-1), L0_ffn_gate_w, L0_ffn_gate_b, L0_ffn_expert_bias, L0_ffn_w_gate_up, L0_ffn_w_down)
    return h

_drawn_inputs = setup_inputs


def setup_inputs(seed=0):
    import zlib

    import numpy as np

    out = dict(_drawn_inputs(seed))
    spreads = {'L0_attn_b_qkv': (0.0, 0.1), 'L0_attn_b_out': (0.0, 0.1), 'L0_ffn_gate_b': (0.0, 0.8)}
    factors = {'L0_tok_norm_weight': 5.666,
     'L0_ffn_gate_w': 4.07,
     'L0_ffn_expert_bias': 8.0,
     'L0_ffn_w_gate_up': 3.352,
     'L0_ffn_w_down': 3.355}
    for name, (base, spread) in spreads.items():
        noise = np.random.default_rng([zlib.crc32(name.encode()), seed]).standard_normal(out[name].shape)
        drawn = base * np.exp(spread * noise) if base else spread * noise
        out[name] = jnp.asarray(drawn.astype(out[name].dtype))
    for name, factor in factors.items():
        out[name] = (out[name] * factor).astype(out[name].dtype)
    return out
```

```python
from contextlib import ExitStack

import concourse.bass as bass
from concourse import mybir

F32 = mybir.dt.float32
F32R = mybir.dt.float32r
I32 = mybir.dt.int32
ALU = mybir.AluOpType
ACT = mybir.ActivationFunctionType
AX = mybir.AxisListType

P = 128
BANK = 512
RMS_EPS = 1e-6
LN_EPS = 1e-5
ABSENT = -1e30
NO_EXPERT = -3e38
TAKEN = -1e38


def tower_program(nc, ids, emb, embT, cols, rows, projT, wqkvT, woT, gate_up, down, out):
    T = out.shape[0]
    D = emb.shape[1]
    DC = D // P
    TB = T // P
    EXPERTS, HALVES, _, _, _, HALF = gate_up.shape
    STEPS = EXPERTS * HALVES
    SPP = 2 * HALVES
    PAIRS = STEPS // SPP
    CHUNKS = SPP * HALF // P
    EDGE = [(s * HALF) // P for s in range(SPP + 1)]
    GROUP = [(EDGE[s], EDGE[s + 1]) for s in range(SPP)]
    GMAX = max(b - a for a, b in GROUP)
    GU = DC * 2 * HALF
    SCALE = float(D) ** -0.5
    assert emb.shape[0] == P and T % P == 0 and HALF * SPP == CHUNKS * P and D == BANK
    NW, BQKV, GW = 0, DC, DC + 3 * DC
    BO, GB, EB = 0, D, D + EXPERTS

    with ExitStack() as ctx:
        def sb(name, shape, dt=F32):
            return ctx.enter_context(nc.sbuf_tensor(name, shape, dt))

        def sem(name):
            return ctx.enter_context(nc.semaphore(name))

        raw_gu = sb("raw_gu", [P, SPP, GU])
        raw_dn = sb("raw_dn", [P, CHUNKS, D])
        gu_hi = sb("gu_hi", [P, 2, DC, 2, HALF], F32R)
        gu_lo = sb("gu_lo", [P, 2, DC, 2, HALF], F32R)
        dn_hi = sb("dn_hi", [P, 2, GMAX, D], F32R)
        dn_lo = sb("dn_lo", [P, 2, GMAX, D], F32R)
        onehot = sb("onehot", [P, T], F32R)
        wv = sb("wv", [P, DC, D])
        wo = sb("wo", [P, DC, D])
        row_select = raw_gu[:, 1, 0:TB * P].rearrange("p (j i) -> p j i", j=TB)
        wq = raw_gu[:, 2, 0:DC * D].rearrange("p (c o) -> p c o", c=DC)
        embT_sb = raw_gu[:, 2, DC * D:DC * D + DC * P].rearrange("p (c v) -> p c v", c=DC)
        proj_sb = raw_gu[:, 3, 0:DC * D].rearrange("p (c o) -> p c o", c=DC)
        emb_sb = raw_gu[:, 3, DC * D:DC * D + D]
        late = raw_dn[:, GROUP[2][0]:, :].rearrange("p c d -> p (c d)")
        wk = late[:, 0:DC * D].rearrange("p (c o) -> p c o", c=DC)
        embT_w = late[:, DC * D:DC * D + DC * P].rearrange("p (c v) -> p c v", c=DC)
        count_scratch = raw_gu[:, 1, 0:T]
        out_sb = raw_gu[:, :, :].rearrange("p s n -> p (s n)")[:, 0:TB * D].rearrange("p (j d) -> p j d", j=TB)

        cols_sb = sb("cols_sb", [P, cols.shape[1]])
        rows_sb = sb("rows_sb", [P, rows.shape[1]])
        ids_sb = sb("ids_sb", [TB, P], I32)
        ids_f = sb("ids_f", [TB, 3, P])
        ident = sb("ident", [P, P])
        row_index = sb("row_index", [P, 1])
        exponent = sb("exponent", [P, 2])
        count = sb("count", [P, 1])
        count_wide = sb("count_wide", [P, P])
        count_row = sb("count_row", [P, P])
        absent_row = sb("absent_row", [P, P])
        stat = sb("stat", [P, 64])
        h = sb("h", [P, D])
        hb = sb("hb", [P, D])
        x1 = sb("x1", [P, D])
        x1T = sb("x1T", [P, DC, P])
        qkvT = sb("qkvT", [P, 3, DC, P])
        vo = sb("vo", [P, D])
        score = sb("score", [P, P])
        prob = sb("prob", [P, P])
        probT = sb("probT", [P, P])
        h2 = sb("h2", [P, D])
        x2T_hi = sb("x2T_hi", [P, DC, P], F32R)
        x2T_lo = sb("x2T_lo", [P, DC, P], F32R)
        router = sb("router", [P, 8, 16])
        silu = sb("silu", [P, 2, HALF])
        interT_hi = sb("interT_hi", [P, 2, GMAX, P], F32R)
        interT_lo = sb("interT_lo", [P, 2, GMAX, P], F32R)
        row_hi = sb("row_hi", [P, D], F32R)
        row_lo = sb("row_lo", [P, D], F32R)
        x2 = x1
        inter = qkvT[:, :, :, :].rearrange("p a c v -> p (a c v)")[:, 0:SPP * HALF]
        row = x1T[:, :, :].rearrange("p c v -> p (c v)")

        def st(i, n=1):
            return stat[:, i:i + n]

        sumsq, c0, bn, mv, v0, u2, scales, nmax, rsum, rinv = (
            st(0), st(1), st(2, 6), st(8, 2), st(10), st(12, 2), st(14, 2), st(16), st(17), st(18))
        bn2, mv2, u3, k2, lmax, lsum, linv = st(20, 6), st(26, 2), st(28), st(29), st(30), st(31), st(32)
        mean, var, s_h, k_x1 = mv[:, 0:1], mv[:, 1:2], scales[:, 0:1], scales[:, 1:2]
        logits, expd, routing, top, marked, comb = (router[:, i, :] for i in range(6))

        ps_gu = ctx.enter_context(nc.psum_tensor("ps_gu", [P, 4, BANK], F32))
        ps_t = ctx.enter_context(nc.psum_tensor("ps_t", [P, 2, BANK], F32))
        ps_x = ctx.enter_context(nc.psum_tensor("ps_x", [P, BANK], F32))
        ps_acc = ctx.enter_context(nc.psum_tensor("ps_acc", [P, BANK], F32))
        gather_bank = [ps_gu[:, 0], ps_gu[:, 1], ps_gu[:, 2], ps_gu[:, 3], ps_t[:, 0], ps_t[:, 1], ps_x[:], ps_acc[:]]

        ids_in, cols_in, rows_in, emb_in, embT_in, proj_in = (
            sem(n) for n in ("ids_in", "cols_in", "rows_in", "emb_in", "embT_in", "proj_in"))
        wq_in, wk_in, wv_in, wo_in = (sem(n) for n in ("wq_in", "wk_in", "wv_in", "wo_in"))
        gu_in = [sem(f"gu_in{s}") for s in range(SPP)]
        dn_in = [sem(f"dn_in{s}") for s in range(SPP)]
        zeroed, consts = sem("zeroed"), sem("consts")
        ids_fixed, ids_spread, onehot_ready = sem("ids_fixed"), sem("ids_spread"), sem("onehot_ready")
        counted, count_widened, count_spread, counts_ready = (
            sem(n) for n in ("counted", "count_widened", "count_spread", "counts_ready"))
        emb_squared, embT_scaled, projected = sem("emb_squared"), sem("embT_scaled"), sem("projected")
        moments, small_done, scales_ready = sem("moments"), sem("small_done"), sem("scales_ready")
        x1_ready, h_ready, hb_ready, x1_turned, x1T_ready = (
            sem(n) for n in ("x1_ready", "h_ready", "hb_ready", "x1_turned", "x1T_ready"))
        qkv_done, q_ready, k_ready, v_ready = (sem(n) for n in ("qkv_done", "q_ready", "k_ready", "v_ready"))
        scored, softmax_step, exp_ready, prob_ready = (
            sem(n) for n in ("scored", "softmax_step", "exp_ready", "prob_ready"))
        vo_done, vo_ready, prob_turned, probT_ready, attended = (
            sem(n) for n in ("vo_done", "vo_ready", "prob_turned", "probT_ready", "attended"))
        h2_ready, moments2, k2_ready, x2_ready, x2_turned, x2T_hi_ready, x2T_lo_ready = (
            sem(n) for n in ("h2_ready", "moments2", "k2_ready", "x2_ready", "x2_turned",
                             "x2T_hi_ready", "x2T_lo_ready"))
        routed, router_step, lexp_ready = sem("routed"), sem("router_step"), sem("lexp_ready")
        gu_hi_done, gu_lo_done = sem("gu_hi_done"), sem("gu_lo_done")
        dn_hi_done, dn_lo_done = sem("dn_hi_done"), sem("dn_lo_done")
        gu_summed, silu_done, inter_done = sem("gu_summed"), sem("silu_done"), sem("inter_done")
        turned, turned_hi, turned_lo, down_summed = (
            sem(n) for n in ("turned", "turned_hi", "turned_lo", "down_summed"))
        row_ready, row_hi_ready, row_lo_ready = sem("row_ready"), sem("row_hi_ready"), sem("row_lo_ready")
        gathered, even_out, odd_out, stored = sem("gathered"), sem("even_out"), sem("odd_out"), sem("stored")

        def pair_wait(eng, semaphore, pair, per_pair, at_first):
            if isinstance(pair, int) and pair == 0 and at_first <= 0:
                return
            eng.wait_ge(semaphore, pair * per_pair + at_first)

        def over_pairs(eng, steps):
            steps(0)
            for pair in range(1, PAIRS):
                steps(pair)

        block = ctx.enter_context(nc.Block())

        @block.sync
        def _(sp):
            sp.dma_start(ids_sb[:], ids).then_inc(ids_in, 16)
            sp.dma_start(cols_sb[:], cols).then_inc(cols_in, 16)
            sp.dma_start(embT_sb, embT).then_inc(embT_in, 16)
            sp.dma_start(proj_sb, projT).then_inc(proj_in, 16)
            sp.dma_start(emb_sb, emb).then_inc(emb_in, 16)
            for part, (dst, landed) in enumerate(((wq, wq_in), (wk, wk_in), (wv[:], wv_in))):
                sp.dma_start(dst, wqkvT[part]).then_inc(landed, 16)
            sp.dma_start(wo[:], woT).then_inc(wo_in, 16)
            sp.dma_start(rows_sb[:], rows.to_broadcast([P, rows.shape[1]])).then_inc(rows_in, 16)

            def load_pair(pair):
                for s in range(SPP):
                    a, b = GROUP[s]
                    if isinstance(pair, int) and pair == 0:
                        if s == 1:
                            sp.wait_ge(counted, 1)
                        if s == 2:
                            sp.wait_ge(qkv_done, 1)
                            sp.wait_ge(embT_scaled, 1)
                        if s == 3:
                            sp.wait_ge(projected, 1)
                            sp.wait_ge(emb_squared, 1)
                    pair_wait(sp, gu_hi_done, pair, SPP * DC, (s + 1 - SPP) * DC)
                    pair_wait(sp, gu_lo_done, pair, SPP * DC, (s + 1 - SPP) * DC)
                    sp.dma_start(raw_gu[:, s, :], gate_up_rows[pair * SPP + s]).then_inc(gu_in[s], 16)
                    if isinstance(pair, int) and pair == 0 and s >= 2:
                        sp.wait_ge(qkv_done, 2)
                        sp.wait_ge(projected, 1)
                    pair_wait(sp, dn_hi_done, pair, SPP, s + 1 - SPP)
                    pair_wait(sp, dn_lo_done, pair, SPP, s + 1 - SPP)
                    sp.dma_start(raw_dn[:, a:b, :], down[pair, :, a:b, :]).then_inc(dn_in[s], 16)

            gate_up_rows = gate_up.rearrange("e h p c g n -> (e h) p (c g n)")
            over_pairs(sp, load_pair)

            out_rows = out.rearrange("(p j) d -> p j d", j=TB)
            for j in range(0, TB, 2):
                sp.wait_ge(even_out, j // 2 + 1)
                sp.wait_ge(odd_out, j // 2 + 1)
                sp.dma_start(out_rows[:, j:j + 2, :], out_sb[:, j:j + 2, :]).then_inc(stored, 16)
            sp.wait_ge(stored, 16 * (TB // 2))

        @block.gpsimd
        def _(pool):
            pool.memset(row_select[0:TB], 0.0).then_inc(zeroed, 1)
            pool.memset(ident[:], 0.0).then_inc(zeroed, 1)
            pool.memset(exponent[:], -0.5).then_inc(consts, 1)
            pool.iota(row_index[:], [[0, 1]], base=0, channel_multiplier=1,
                      allow_small_or_imprecise_dtypes=True).then_inc(consts, 1)
            pool.wait_ge(zeroed, 2)
            pool.affine_select(out=row_select[0:TB], in_=row_select[0:TB], compare_op=ALU.not_equal, fill=1.0,
                               base=0, pattern=[[-1, TB], [0, P]], channel_multiplier=1).then_inc(consts, 1)
            pool.affine_select(out=ident[:], in_=ident[:], compare_op=ALU.not_equal, fill=1.0,
                               base=0, pattern=[[-1, P]], channel_multiplier=1).then_inc(consts, 1)
            pool.wait_ge(emb_squared, 1)
            pool.tensor_scalar(c0, sumsq, RMS_EPS / D, RMS_EPS * RMS_EPS, ALU.mult, ALU.add).then_inc(small_done, 1)
            pool.wait_ge(small_done, 1)
            pool.wait_ge(moments, 2)
            pool.tensor_tensor(v0, var, c0, ALU.add).then_inc(small_done, 1)
            pool.wait_ge(small_done, 2)
            pool.tensor_scalar(u2[:, 0:1], mean, mean, v0, ALU.mult, ALU.add).then_inc(small_done, 1)
            pool.wait_ge(small_done, 3)
            pool.tensor_scalar(u2[:, 1:2], u2[:, 0:1], LN_EPS, var, ALU.mult, ALU.add).then_inc(small_done, 1)
            pool.wait_ge(small_done, 4)
            pool.wait_ge(consts, 4)
            pool.tensor_tensor(scales, u2, exponent[:], ALU.pow).then_inc(scales_ready, 1)
            pool.wait_ge(h_ready, 1)
            pool.wait_ge(rows_in, 16)
            pool.tensor_tensor(hb[:], h[:], rows_sb[:, BO:BO + D], ALU.add).then_inc(hb_ready, 1)

            def split_pair(pair):
                for s in range(SPP):
                    down_lo(pair, s)

            def down_lo(pair, s):
                a, b = GROUP[s]
                buf = s % 2
                pool.wait_ge(dn_in[s], (pair + 1) * 16)
                pair_wait(pool, dn_hi_done, pair, SPP, s + 1)
                pair_wait(pool, down_summed, pair, SPP, s - 1)
                pool.tensor_tensor(dn_lo[:, buf, 0:b - a, :], raw_dn[:, a:b, :],
                                   dn_hi[:, buf, 0:b - a, :].bitcast(F32), ALU.subtract).then_inc(dn_lo_done, 1)

            pool.wait_ge(moments2, 2)
            pool.tensor_scalar(u3, mv2[:, 1:2], LN_EPS, None, ALU.add).then_inc(small_done, 1)
            pool.wait_ge(small_done, 5)
            pool.tensor_tensor(k2, u3, exponent[:, 0:1], ALU.pow).then_inc(k2_ready, 1)
            over_pairs(pool, split_pair)

        @block.scalar
        def _(act):
            def gu_hi_chunk(pair, s, c):
                buf = s % 2
                if c == 0:
                    act.wait_ge(gu_in[s], (pair + 1) * 16)
                    pair_wait(act, gu_summed, pair, SPP, s - 1)
                act.activation(gu_hi[:, buf, c], raw_gu[:, s, c * 2 * HALF:(c + 1) * 2 * HALF]
                               .rearrange("p (g n) -> p g n", g=2), ACT.Copy).then_inc(gu_hi_done, 1)

            def down_hi(pair, s):
                a, b = GROUP[s]
                act.wait_ge(dn_in[s], (pair + 1) * 16)
                pair_wait(act, down_summed, pair, SPP, s - 1)
                act.activation(dn_hi[:, s % 2, 0:b - a, :], raw_dn[:, a:b, :], ACT.Copy).then_inc(dn_hi_done, 1)

            def silu_of(pair, s):
                pair_wait(act, gu_summed, pair, SPP, s + 1)
                pair_wait(act, inter_done, pair, SPP, s - 1)
                act.activation(silu[:, s % 2], ps_gu[:, 2 * (s % 2), 0:HALF], ACT.Silu).then_inc(silu_done, 1)

            def interT_hi_of(pair, s):
                a, b = GROUP[s]
                pair_wait(act, turned, pair, SPP, s + 1)
                pair_wait(act, down_summed, pair, SPP, s - 1)
                act.activation(interT_hi[:, s % 2, 0:b - a, :],
                               ps_t[:, s % 2, 0:(b - a) * P].rearrange("p (c v) -> p c v", v=P),
                               ACT.Copy).then_inc(turned_hi, 1)

            act.wait_ge(emb_in, 16)
            act.activation(hb[:], emb_sb, ACT.Square, accum_out=sumsq).then_inc(emb_squared, 1)
            act.wait_ge(onehot_ready, 4)
            act.activation(count_scratch, onehot[:].bitcast(F32), ACT.Copy, accum_out=count[:]).then_inc(counted, 1)
            act.wait_ge(x1_ready, 1)
            act.activation(h[:], ps_x[:], ACT.Copy, scale=s_h).then_inc(h_ready, 1)
            act.wait_ge(x1_turned, 1)
            act.activation(x1T[:, :, :], ps_t[:, 0].rearrange("p (c v) -> p c v", v=P), ACT.Copy).then_inc(x1T_ready, 1)
            for c in range(DC):
                gu_hi_chunk(0, 0, c)
            act.wait_ge(qkv_done, 3)
            for c in range(DC):
                act.activation(qkvT[:, 2, c], ps_gu[:, 2, c * P:(c + 1) * P], ACT.Identity,
                               bias=cols_sb[:, BQKV + 2 * DC + c:BQKV + 2 * DC + c + 1]).then_inc(v_ready, 1)
            act.wait_ge(softmax_step, 2)
            act.activation(prob[:], score[:], ACT.Exp, bias=nmax).then_inc(exp_ready, 1)
            act.wait_ge(vo_done, 1)
            act.activation(vo[:], ps_gu[:, 3], ACT.Copy).then_inc(vo_ready, 1)
            act.wait_ge(prob_turned, 1)
            act.activation(probT[:], ps_t[:, 0, 0:P], ACT.Copy).then_inc(probT_ready, 1)
            act.wait_ge(x2_turned, 1)
            act.activation(x2T_hi[:, :, :], ps_t[:, 0].rearrange("p (c v) -> p c v", v=P),
                           ACT.Copy).then_inc(x2T_hi_ready, 1)
            act.wait_ge(router_step, 2)
            act.activation(expd[:, 0:EXPERTS], logits[:, 0:EXPERTS], ACT.Exp, bias=lmax,
                           accum_out=lsum).then_inc(lexp_ready, 1)

            def pair_steps(pair):
                for s in range(SPP):
                    first = isinstance(pair, int) and pair == 0
                    if not (first and s < 2):
                        silu_of(*before(pair, s, 2))
                    if not (first and s == 0):
                        gu_hi_chunk(pair, s, 0)
                    if not (first and s < 2):
                        interT_hi_of(*before(pair, s, 2))
                    if not (first and s == 0):
                        for c in range(1, DC):
                            gu_hi_chunk(pair, s, c)
                        down_hi(*before(pair, s, 1))

            over_pairs(act, pair_steps)
            last = SPP - 1
            silu_of(PAIRS - 1, last - 1)
            interT_hi_of(PAIRS - 1, last - 1)
            down_hi(PAIRS - 1, last)
            silu_of(PAIRS - 1, last)
            interT_hi_of(PAIRS - 1, last)
            act.wait_ge(row_ready, 1)
            act.activation(row_hi[:], row, ACT.Copy).then_inc(row_hi_ready, 1)
            for j in range(0, TB, 2):
                act.wait_ge(gathered, j + 1)
                act.activation(out_sb[:, j, :], gather_bank[j % 8], ACT.Copy).then_inc(even_out, 1)

        @block.vector
        def _(dve):
            def gu_lo_chunk(pair, s, c):
                buf = s % 2
                if c == 0:
                    dve.wait_ge(gu_in[s], (pair + 1) * 16)
                    pair_wait(dve, gu_summed, pair, SPP, s - 1)
                pair_wait(dve, gu_hi_done, pair, SPP * DC, s * DC + c + 1)
                dve.tensor_tensor(gu_lo[:, buf, c], raw_gu[:, s, c * 2 * HALF:(c + 1) * 2 * HALF]
                                  .rearrange("p (g n) -> p g n", g=2),
                                  gu_hi[:, buf, c].bitcast(F32), ALU.subtract).then_inc(gu_lo_done, 1)

            def inter_of(pair, s):
                if isinstance(pair, int):
                    e = pair * 2 + s // HALVES
                    weight = comb[:, e:e + 1]
                else:
                    weight = comb[:, bass.ds(pair * 2 + s // HALVES, 1)]
                pair_wait(dve, silu_done, pair, SPP, s + 1)
                pair_wait(dve, turned, pair, SPP, s - 2)
                dve.scalar_tensor_tensor(out=inter[:, s * HALF:(s + 1) * HALF], in0=silu[:, s % 2], scalar=weight,
                                         in1=ps_gu[:, 2 * (s % 2) + 1, 0:HALF], op0=ALU.mult,
                                         op1=ALU.mult).then_inc(inter_done, 1)

            def interT_lo_of(pair, s):
                a, b = GROUP[s]
                pair_wait(dve, turned_hi, pair, SPP, s + 1)
                pair_wait(dve, down_summed, pair, SPP, s - 1)
                dve.tensor_tensor(interT_lo[:, s % 2, 0:b - a, :],
                                  ps_t[:, s % 2, 0:(b - a) * P].rearrange("p (c v) -> p c v", v=P),
                                  interT_hi[:, s % 2, 0:b - a, :].bitcast(F32), ALU.subtract).then_inc(turned_lo, 1)

            dve.wait_ge(ids_in, 16)
            dve.tensor_scalar(ids_f[:, 0], ids_sb[:], 0.0, float(P), ALU.is_lt, ALU.mult).then_inc(ids_fixed, 1)
            dve.wait_ge(ids_fixed, 1)
            dve.tensor_tensor(ids_f[:, 1], ids_f[:, 0], ids_sb[:], ALU.add).then_inc(ids_fixed, 1)
            dve.wait_ge(ids_fixed, 2)
            dve.tensor_scalar(ids_f[:, 2], ids_f[:, 1], 0.0, float(P - 1), ALU.max, ALU.min).then_inc(ids_fixed, 1)
            dve.wait_ge(embT_in, 16)
            dve.wait_ge(cols_in, 16)
            dve.tensor_tensor(embT_w, embT_sb, cols_sb[:, NW:NW + DC, None].to_broadcast([P, DC, P]),
                              ALU.mult).then_inc(embT_scaled, 1)
            dve.wait_ge(ids_spread, 1)
            dve.wait_ge(consts, 4)
            for b in range(4):
                dve.tensor_scalar(onehot[:, b * BANK:(b + 1) * BANK], ps_gu[:, b], row_index[:], None,
                                  ALU.is_equal).then_inc(onehot_ready, 1)
            dve.wait_ge(projected, 1)
            dve.bn_stats(bn, ps_x[:]).then_inc(moments, 1)
            dve.wait_ge(moments, 1)
            dve.bn_aggr(mv, bn).then_inc(moments, 1)
            dve.wait_ge(counted, 1)
            dve.tensor_copy(count_wide[:], count[:, 0:1].to_broadcast([P, P])).then_inc(count_widened, 1)
            dve.wait_ge(moments, 2)
            dve.wait_ge(scales_ready, 1)
            dve.tensor_scalar(x1[:], ps_x[:], mean, k_x1, ALU.subtract, ALU.mult).then_inc(x1_ready, 1)
            dve.wait_ge(count_spread, 1)
            dve.tensor_copy(count_row[:], ps_t[:, 1, 0:P]).then_inc(counts_ready, 1)
            dve.tensor_scalar(absent_row[:], ps_t[:, 1, 0:P], 0.0, ABSENT, ALU.is_equal,
                              ALU.mult).then_inc(counts_ready, 1)
            for part, ready in ((0, q_ready), (1, k_ready)):
                dve.wait_ge(qkv_done, part + 1)
                bias = cols_sb[:, BQKV + part * DC:BQKV + (part + 1) * DC, None].to_broadcast([P, DC, P])
                dve.tensor_tensor(qkvT[:, part], ps_gu[:, part].rearrange("p (c v) -> p c v", v=P), bias,
                                  ALU.add).then_inc(ready, 1)
            dve.wait_ge(scored, 1)
            dve.wait_ge(counts_ready, 2)
            dve.scalar_tensor_tensor(out=score[:], in0=ps_t[:, 1, 0:P], scalar=SCALE, in1=absent_row[:],
                                     op0=ALU.mult, op1=ALU.add).then_inc(softmax_step, 1)
            dve.wait_ge(softmax_step, 1)
            dve.tensor_reduce(nmax, score[:], AX.X, ALU.max, negate=True).then_inc(softmax_step, 1)
            dve.wait_ge(exp_ready, 1)
            dve.scalar_tensor_tensor(out=score[:], in0=prob[:], scalar=1.0, in1=count_row[:], op0=ALU.mult,
                                     op1=ALU.mult, accum_out=rsum).then_inc(prob_ready, 1)
            dve.wait_ge(prob_ready, 1)
            dve.reciprocal(rinv, rsum).then_inc(softmax_step, 1)
            for c in range(DC):
                gu_lo_chunk(0, 0, c)
            dve.wait_ge(attended, 1)
            dve.wait_ge(softmax_step, 3)
            dve.wait_ge(hb_ready, 1)
            dve.scalar_tensor_tensor(out=h2[:], in0=ps_x[:], scalar=rinv, in1=hb[:], op0=ALU.mult,
                                     op1=ALU.add).then_inc(h2_ready, 1)
            dve.wait_ge(h2_ready, 1)
            dve.bn_stats(bn2, h2[:]).then_inc(moments2, 1)
            dve.wait_ge(moments2, 1)
            dve.bn_aggr(mv2, bn2).then_inc(moments2, 1)
            dve.wait_ge(moments2, 2)
            dve.wait_ge(k2_ready, 1)
            dve.tensor_scalar(x2[:], h2[:], mv2[:, 0:1], k2, ALU.subtract, ALU.mult).then_inc(x2_ready, 1)
            dve.wait_ge(x2T_hi_ready, 1)
            dve.tensor_tensor(x2T_lo[:, :, :], ps_t[:, 0].rearrange("p (c v) -> p c v", v=P),
                              x2T_hi[:, :, :].bitcast(F32), ALU.subtract).then_inc(x2T_lo_ready, 1)
            dve.memset(routing, NO_EXPERT).then_inc(router_step, 1)
            dve.wait_ge(routed, 1)
            dve.tensor_tensor(logits[:, 0:EXPERTS], ps_t[:, 1, 0:EXPERTS], rows_sb[:, GB:GB + EXPERTS],
                              ALU.add).then_inc(routed, 1)
            dve.wait_ge(routed, 2)
            dve.tensor_reduce(lmax, logits[:, 0:EXPERTS], AX.X, ALU.max, negate=True).then_inc(router_step, 1)
            dve.wait_ge(lexp_ready, 1)
            dve.reciprocal(linv, lsum).then_inc(router_step, 1)
            dve.wait_ge(router_step, 3)
            dve.scalar_tensor_tensor(out=routing[:, 0:EXPERTS], in0=expd[:, 0:EXPERTS], scalar=linv,
                                     in1=rows_sb[:, EB:EB + EXPERTS], op0=ALU.mult,
                                     op1=ALU.add).then_inc(router_step, 1)
            dve.wait_ge(router_step, 4)
            dve.max(top[:, 0:8], routing).then_inc(router_step, 1)
            dve.wait_ge(router_step, 5)
            dve.memset(top[:, 2:8], NO_EXPERT).then_inc(router_step, 1)
            dve.wait_ge(router_step, 6)
            dve.match_replace(marked, top[:, 0:8], routing, TAKEN).then_inc(router_step, 1)
            dve.wait_ge(router_step, 7)
            dve.scalar_tensor_tensor(out=comb[:, 0:EXPERTS], in0=marked[:, 0:EXPERTS], scalar=TAKEN / 2,
                                     in1=routing[:, 0:EXPERTS], op0=ALU.is_lt, op1=ALU.mult).then_inc(router_step, 1)
            dve.wait_ge(router_step, 8)

            def pair_steps(pair):
                for s in range(SPP):
                    first = isinstance(pair, int) and pair == 0
                    if not (first and s < 2):
                        inter_of(*before(pair, s, 2))
                    if not (first and s == 0):
                        gu_lo_chunk(pair, s, 0)
                    if not (first and s < 2):
                        interT_lo_of(*before(pair, s, 2))
                    if not (first and s == 0):
                        for c in range(1, DC):
                            gu_lo_chunk(pair, s, c)

            over_pairs(dve, pair_steps)
            last = SPP - 1
            inter_of(PAIRS - 1, last - 1)
            interT_lo_of(PAIRS - 1, last - 1)
            inter_of(PAIRS - 1, last)
            interT_lo_of(PAIRS - 1, last)
            dve.wait_ge(down_summed, STEPS)
            dve.tensor_tensor(row, ps_acc[:], h2[:], ALU.add).then_inc(row_ready, 1)
            dve.wait_ge(row_hi_ready, 1)
            dve.tensor_tensor(row_lo[:], row, row_hi[:].bitcast(F32), ALU.subtract).then_inc(row_lo_ready, 1)
            for j in range(1, TB, 2):
                dve.wait_ge(gathered, j + 1)
                dve.tensor_copy(out_sb[:, j, :], gather_bank[j % 8]).then_inc(odd_out, 1)

        @block.tensor
        def _(pe):
            def turn(dst, src, done):
                for c in range(DC):
                    ins = pe.transpose(dst[:, c * P:(c + 1) * P], src[:, c * P:(c + 1) * P], ident[:])
                ins.then_inc(done, 1)

            pe.wait_ge(ids_fixed, 3)
            pe.wait_ge(consts, 4)
            for j in range(TB):
                ins = pe.matmul(ps_gu[:, j // 4, (j % 4) * P:(j % 4 + 1) * P], row_select[0:TB, j, :], ids_f[:, 2],
                                start=True, stop=True)
            ins.then_inc(ids_spread, 1)
            pe.wait_ge(embT_scaled, 1)
            pe.wait_ge(proj_in, 16)
            for c in range(DC):
                ins = pe.matmul(ps_x[:], embT_w[:, c], proj_sb[:, c], start=(c == 0), stop=(c == DC - 1))
            ins.then_inc(projected, 1)
            pe.wait_ge(count_widened, 1)
            pe.matmul(ps_t[:, 1, 0:P], count_wide[:], ident[:], start=True, stop=True).then_inc(count_spread, 1)
            pe.wait_ge(x1_ready, 1)
            turn(ps_t[:, 0], x1[:], x1_turned)
            pe.wait_ge(x1T_ready, 1)
            pe.wait_ge(onehot_ready, 4)
            for part, (weights, landed) in enumerate(((wq, wq_in), (wk, wk_in), (wv[:], wv_in))):
                pe.wait_ge(landed, 16)
                for o in range(DC):
                    for c in range(DC):
                        ins = pe.matmul(ps_gu[:, part, o * P:(o + 1) * P], weights[:, c, o * P:(o + 1) * P],
                                        x1T[:, c], start=(c == 0), stop=(c == DC - 1))
                ins.then_inc(qkv_done, 1)
            pe.wait_ge(q_ready, 1)
            pe.wait_ge(k_ready, 1)
            pe.wait_ge(counts_ready, 2)
            for c in range(DC):
                ins = pe.matmul(ps_t[:, 1, 0:P], qkvT[:, 0, c], qkvT[:, 1, c], start=(c == 0), stop=(c == DC - 1))
            ins.then_inc(scored, 1)
            pe.wait_ge(wo_in, 16)
            pe.wait_ge(v_ready, DC)
            for c in range(DC):
                ins = pe.matmul(ps_gu[:, 3], qkvT[:, 2, c], wo[:, c], start=(c == 0), stop=(c == DC - 1))
            ins.then_inc(vo_done, 1)
            pe.wait_ge(prob_ready, 1)
            pe.transpose(ps_t[:, 0, 0:P], score[:], ident[:]).then_inc(prob_turned, 1)
            pe.wait_ge(probT_ready, 1)
            pe.wait_ge(vo_ready, 1)
            pe.wait_ge(h_ready, 1)
            pe.matmul(ps_x[:], probT[:], vo[:], start=True, stop=True).then_inc(attended, 1)
            pe.wait_ge(x2_ready, 1)
            turn(ps_t[:, 0], x2, x2_turned)

            def route():
                n = 0
                for xT in (x2T_hi, x2T_lo):
                    for c in range(DC):
                        ins = pe.matmul(ps_t[:, 1, 0:EXPERTS], xT[:, c].bitcast(F32),
                                        cols_sb[:, GW + c * EXPERTS:GW + (c + 1) * EXPERTS],
                                        start=(n == 0), stop=(n == 2 * DC - 1))
                        n += 1
                ins.then_inc(routed, 1)

            def gate_up_sum(pair, s, chunks):
                buf = s % 2
                if 0 in chunks:
                    pair_wait(pe, silu_done, pair, SPP, s - 1)
                    pair_wait(pe, inter_done, pair, SPP, s - 1)
                for c in chunks:
                    pair_wait(pe, gu_hi_done, pair, SPP * DC, s * DC + c + 1)
                    pair_wait(pe, gu_lo_done, pair, SPP * DC, s * DC + c + 1)
                    for n, (x, w) in enumerate(((x2T_hi, gu_hi), (x2T_hi, gu_lo), (x2T_lo, gu_hi))):
                        for g in range(2):
                            ins = pe.matmul(ps_gu[:, 2 * buf + g, 0:HALF], x[:, c], w[:, buf, c, g],
                                            start=(c == 0 and n == 0), stop=(c == DC - 1 and n == 2))
                if DC - 1 in chunks:
                    ins.then_inc(gu_summed, 1)

            def turn_inter(pair, s):
                a, b = GROUP[s]
                pair_wait(pe, inter_done, pair, SPP, s + 1)
                pair_wait(pe, turned_lo, pair, SPP, s - 1)
                for c in range(a, b):
                    ins = pe.transpose(ps_t[:, s % 2, (c - a) * P:(c - a + 1) * P],
                                       inter[:, c * P:(c + 1) * P], ident[:])
                ins.then_inc(turned, 1)

            def down_sum(pair, s, first=False, last=False):
                a, b = GROUP[s]
                buf = s % 2
                pair_wait(pe, turned_hi, pair, SPP, s + 1)
                pair_wait(pe, dn_hi_done, pair, SPP, s + 1)
                pair_wait(pe, turned_lo, pair, SPP, s + 1)
                pair_wait(pe, dn_lo_done, pair, SPP, s + 1)
                for c in range(b - a):
                    for n, (x, w) in enumerate(((interT_hi, dn_hi), (interT_hi, dn_lo), (interT_lo, dn_hi))):
                        ins = pe.matmul(ps_acc[:], x[:, buf, c], w[:, buf, c], start=(first and c == 0 and n == 0),
                                        stop=(last and c == b - a - 1 and n == 2))
                ins.then_inc(down_summed, 1)

            pe.wait_ge(x2T_hi_ready, 1)
            pe.wait_ge(x2T_lo_ready, 1)

            def pair_steps(pair):
                for s in range(SPP):
                    first = isinstance(pair, int) and pair == 0
                    gate_up_sum(pair, s, range(0, DC // 2))
                    if first and s == 0:
                        route()
                    else:
                        turn_inter(*before(pair, s, 1))
                    gate_up_sum(pair, s, range(DC // 2, DC))
                    if not (first and s == 0):
                        down_sum(*before(pair, s, 1), first=(first and s == 1))

            over_pairs(pe, pair_steps)
            turn_inter(PAIRS - 1, SPP - 1)
            down_sum(PAIRS - 1, SPP - 1, last=True)
            for j in range(TB):
                if j == 0:
                    pe.wait_ge(row_hi_ready, 1)
                if j >= 8:
                    pe.wait_ge(even_out if j % 2 == 0 else odd_out, j // 2 - 3)
                pe.matmul(gather_bank[j % 8], onehot[:, j * P:(j + 1) * P], row_hi[:], start=True, stop=False)
                if j == 0:
                    pe.wait_ge(row_lo_ready, 1)
                pe.matmul(gather_bank[j % 8], onehot[:, j * P:(j + 1) * P], row_lo[:], start=False,
                          stop=True).then_inc(gathered, 1)


def before(pair, s, n, steps=4):
    return (pair, s - n) if s >= n else (pair - 1, s - n + steps)


def kernel(**inputs):
    import numpy as np
    import concourse.bacc as bacc
    from concourse.bass_utils import run_bass_kernel_spmd

    a = {k: np.asarray(v) for k, v in inputs.items()}
    x, emb = a["x"], a["L0_tok_emb_table"]
    T, D = x.shape[1], emb.shape[1]
    DC, TB = D // P, T // P
    w_gu, w_dn = a["L0_ffn_w_gate_up"], a["L0_ffn_w_down"]
    E, I = w_gu.shape[0], w_dn.shape[2]
    H = 2
    half = I // H

    def chunked(m):
        return m.reshape(DC, P, m.shape[1]).transpose(1, 0, 2)

    def column(v):
        return v.reshape(-1, P).T

    data = {
        "ids": x.reshape(P, TB).T,
        "emb": emb,
        "embT": chunked(emb.T),
        "cols": np.concatenate([column(a["L0_tok_norm_weight"]), column(a["L0_attn_b_qkv"]),
                                chunked(a["L0_ffn_gate_w"].T).reshape(P, DC * E)], axis=1),
        "rows": np.concatenate([a["L0_attn_b_out"], a["L0_ffn_gate_b"], a["L0_ffn_expert_bias"]])[None, :],
        "projT": chunked(a["L0_tok_proj_weight"].T),
        "wqkvT": np.stack([chunked(w.T) for w in np.split(a["L0_attn_w_qkv"], 3)]),
        "woT": chunked(a["L0_attn_w_out"].T),
        "gate_up": w_gu.reshape(E, 2, H, half, DC, P).transpose(0, 2, 5, 4, 1, 3),
        "down": w_dn.transpose(0, 2, 1).reshape(E // 2, 2 * I // P, P, D).transpose(0, 2, 1, 3),
    }
    data = {k: np.ascontiguousarray(v) for k, v in data.items()}
    nc = bacc.Bacc("TRN2", target_bir_lowering=False, num_devices=1)
    aps = [nc.dram_tensor(k, v.shape, mybir.dt.from_np(v.dtype), kind="ExternalInput").ap() for k, v in data.items()]
    out = nc.dram_tensor("out", (T, D), F32, kind="ExternalOutput").ap()
    tower_program(nc, *aps, out)
    result = run_bass_kernel_spmd(nc, [data], core_ids=[0])
    return result.results[0]["out"].reshape(1, T, D)
```

```python
from contextlib import ExitStack

import concourse.bass as bass
from concourse import mybir

F32 = mybir.dt.float32
F32R = mybir.dt.float32r
I32 = mybir.dt.int32
BF16 = mybir.dt.bfloat16
ALU = mybir.AluOpType
ACT = mybir.ActivationFunctionType
AX = mybir.AxisListType

P = 128
BANK = 512
RMS_EPS = 1e-6
LN_EPS = 1e-5
ABSENT = -1e30
NO_EXPERT = -3e38
TAKEN = -1e38
WARM_UP = 9


def tower_program(nc, ids, emb, embT, cols, rows, projT, wqkvT, woT, gate_up, down, out):
    T = out.shape[0]
    D = emb.shape[1]
    DC = D // P
    TB = T // P
    EXPERTS, HALVES, _, _, _, HALF = gate_up.shape
    STEPS = EXPERTS * HALVES
    SPP = 2 * HALVES
    PAIRS = STEPS // SPP
    CHUNKS = SPP * HALF // P
    EDGE = [(s * HALF) // P for s in range(SPP + 1)]
    GROUP = [(EDGE[s], EDGE[s + 1]) for s in range(SPP)]
    GMAX = max(b - a for a, b in GROUP)
    GU = DC * 2 * HALF
    SCALE = float(D) ** -0.5
    assert emb.shape[0] == P and T % P == 0 and HALF * SPP == CHUNKS * P and D == BANK
    NW, BQKV, GW = 0, DC, DC + 3 * DC
    BO, GB, EB = 0, D, D + EXPERTS

    with ExitStack() as ctx:
        def sb(name, shape, dt=F32):
            return ctx.enter_context(nc.sbuf_tensor(name, shape, dt))

        def sem(name):
            return ctx.enter_context(nc.semaphore(name))

        raw_gu = sb("raw_gu", [P, SPP, GU])
        raw_dn = sb("raw_dn", [P, CHUNKS, D])
        gu_hi = sb("gu_hi", [P, 2, DC, 2, HALF + EXPERTS], F32R)
        gu_lo = sb("gu_lo", [P, 2, DC, 2, HALF + EXPERTS], F32R)
        dn_hi = sb("dn_hi", [P, 2, GMAX, D], F32R)
        dn_lo = sb("dn_lo", [P, 2, GMAX, D], F32R)
        onehot = sb("onehot", [P, T], F32R)
        wv = sb("wv", [P, DC, D])
        wo = sb("wo", [P, DC, D])
        ident_b = sb("ident_b", [TB, TB], BF16)
        zeros = sb("zeros", [P, 1], BF16)
        wq = raw_gu[:, 2, 0:DC * D].rearrange("p (c o) -> p c o", c=DC)
        embT_sb = raw_gu[:, 2, DC * D:DC * D + DC * P].rearrange("p (c v) -> p c v", c=DC)
        proj_sb = raw_gu[:, 3, 0:DC * D].rearrange("p (c o) -> p c o", c=DC)
        emb_sb = raw_gu[:, 3, DC * D:DC * D + D]
        late = raw_dn[:, GROUP[2][0]:, :].rearrange("p c d -> p (c d)")
        wk = late[:, 0:DC * D].rearrange("p (c o) -> p c o", c=DC)
        embT_w = late[:, DC * D:DC * D + DC * P].rearrange("p (c v) -> p c v", c=DC)
        BUF = DC * 2 * (HALF + EXPERTS)
        flat = "p a c g n -> p (a c g n)"
        wqkv_hi, wqkv_lo = (
            [gu.rearrange(flat)[:, 0:DC * D], gu.rearrange(flat)[:, BUF:BUF + DC * D],
             dn.rearrange("p a c d -> p (a c d)")[:, 0:DC * D]]
            for gu, dn in ((gu_hi[:, :, :, :, :], dn_hi[:, :, :, :]), (gu_lo[:, :, :, :, :], dn_lo[:, :, :, :])))
        wqkv_hi, wqkv_lo = ([w.rearrange("p (c o) -> p c o", c=DC) for w in parts] for parts in (wqkv_hi, wqkv_lo))
        out_sb = raw_gu[:, :, :].rearrange("p s n -> p (s n)")[:, 0:TB * D].rearrange("p (j d) -> p j d", j=TB)

        cols_sb = sb("cols_sb", [P, cols.shape[1]])
        gate_w = cols_sb[:, GW:GW + DC * EXPERTS].rearrange("p (c e) -> p c e", c=DC)
        rows_sb = sb("rows_sb", [P, rows.shape[1]])
        ids_sb = sb("ids_sb", [TB, P], I32)
        ids_f = sb("ids_f", [TB, 2, P])
        ids_b = sb("ids_b", [TB, P], BF16)
        ident = sb("ident", [P, P])
        row_index = sb("row_index", [P, 1])
        exponent = sb("exponent", [P, 2])
        counts = sb("counts", [P, DC])
        count = sb("count", [P, 1])
        count_wide = sb("count_wide", [P, P])
        count_row = sb("count_row", [P, P])
        absent_row = sb("absent_row", [P, P])
        stat = sb("stat", [P, 64])
        h = sb("h", [P, D])
        hb = sb("hb", [P, D])
        x1 = sb("x1", [P, D])
        qkv = sb("qkv", [P, 3, D])
        x1T_hi = sb("x1T_hi", [P, DC, P], F32R)
        x1T_lo = sb("x1T_lo", [P, DC, P], F32R)
        qkvT = sb("qkvT", [P, 3, DC, P])
        vo = sb("vo", [P, D])
        score = sb("score", [P, P])
        prob = sb("prob", [P, P])
        probT = sb("probT", [P, P])
        h2 = sb("h2", [P, D])
        x2T_hi, x2T_lo = x1T_hi, x1T_lo
        router = sb("router", [P, 8, 16])
        silu = sb("silu", [P, 2, HALF])
        interT_hi = sb("interT_hi", [P, 2, GMAX, P], F32R)
        interT_lo = sb("interT_lo", [P, 2, GMAX, P], F32R)
        x2 = x1
        inter = qkvT[:, :, :, :].rearrange("p a c v -> p (a c v)")[:, 0:SPP * HALF]
        row = hb
        row_hi, row_lo = (t[:, :, :].rearrange("p c v -> p (c v)") for t in (x2T_hi, x2T_lo))

        def st(i, n=1):
            return stat[:, i:i + n]

        sumsq, c0, bn, mv, v0, u2, scales, nmax, rsum, rinv = (
            st(0), st(1), st(2, 6), st(8, 2), st(10), st(12, 2), st(14, 2), st(16), st(17), st(18))
        bn2, mv2, u3, k2, lmax, lsum, linv = st(20, 6), st(26, 2), st(28), st(29), st(30), st(31), st(32)
        h2_sum, spare = st(33), st(34)
        mean, var, s_h, k_x1 = mv[:, 0:1], mv[:, 1:2], scales[:, 0:1], scales[:, 1:2]
        logits, expd, routing, top, marked, comb = (router[:, i, :] for i in range(6))

        ps_gu = ctx.enter_context(nc.psum_tensor("ps_gu", [P, 4, BANK], F32))
        ps_t = ctx.enter_context(nc.psum_tensor("ps_t", [P, 2, BANK], F32))
        ps_x = ctx.enter_context(nc.psum_tensor("ps_x", [P, BANK], F32))
        ps_acc = ctx.enter_context(nc.psum_tensor("ps_acc", [P, BANK], F32))
        vo_bank = [ps_gu[:, 3, 0:D // 2], ps_acc[:, 0:D // 2]]
        gather_bank = [ps_gu[:, 0], ps_gu[:, 1], ps_gu[:, 2], ps_gu[:, 3], ps_t[:, 0], ps_t[:, 1], ps_x[:], ps_acc[:]]

        ids_in, cols_in, rows_in, emb_in, embT_in = (
            sem(n) for n in ("ids_in", "cols_in", "rows_in", "emb_in", "embT_in"))
        proj_in = [sem(f"proj_in{c}") for c in range(DC)]
        wq_in, wk_in, wv_in, wo_in = (sem(n) for n in ("wq_in", "wk_in", "wv_in", "wo_in"))
        gu_in = [sem(f"gu_in{s}") for s in range(SPP)]
        dn_in = [sem(f"dn_in{s}") for s in range(SPP)]
        zeroed, consts, zeros_ready = sem("zeroed"), sem("consts"), sem("zeros_ready")
        ids_fixed, ids_spread, onehot_ready = sem("ids_fixed"), sem("ids_spread"), sem("onehot_ready")
        counted, count_widened, count_spread, counts_ready = (
            sem(n) for n in ("counted", "count_widened", "count_spread", "counts_ready"))
        emb_squared, embT_scaled, projected = sem("emb_squared"), sem("embT_scaled"), sem("projected")
        moments, c0_ready, scale_step, scales_ready = (
            sem(n) for n in ("moments", "c0_ready", "scale_step", "scales_ready"))
        x1_ready, h_ready, hb_ready, x1_turned, x1T_hi_ready, x1T_lo_ready = (
            sem(n) for n in ("x1_ready", "h_ready", "hb_ready", "x1_turned", "x1T_hi_ready", "x1T_lo_ready"))
        wqkv_hi_done, wqkv_lo_done = sem("wqkv_hi_done"), sem("wqkv_lo_done")
        gate_split = sem("gate_split")
        qkv_done, qkv_ready, q_turned, k_turned, v_turned, q_ready, k_ready, v_ready = (
            sem(n) for n in ("qkv_done", "qkv_ready", "q_turned", "k_turned", "v_turned",
                             "q_ready", "k_ready", "v_ready"))
        scored, softmax_step, exp_ready, prob_ready = (
            sem(n) for n in ("scored", "softmax_step", "exp_ready", "prob_ready"))
        vo_done, vo_ready, prob_turned, probT_ready, attended = (
            sem(n) for n in ("vo_done", "vo_ready", "prob_turned", "probT_ready", "attended"))
        h2_ready, moments2, k2_ready, x2_ready, x2_turned, x2T_hi_ready, x2T_lo_ready = (
            sem(n) for n in ("h2_ready", "moments2", "k2_ready", "x2_ready", "x2_turned",
                             "x2T_hi_ready", "x2T_lo_ready"))
        routed, router_step, lexp_ready, silu_table = (
            sem(n) for n in ("routed", "router_step", "lexp_ready", "silu_table"))
        gu_hi_done, gu_lo_done = sem("gu_hi_done"), sem("gu_lo_done")
        dn_hi_done, dn_lo_done = sem("dn_hi_done"), sem("dn_lo_done")
        gu_summed, silu_done, inter_done = sem("gu_summed"), sem("silu_done"), sem("inter_done")
        turned, turned_hi, turned_lo, down_summed = (
            sem(n) for n in ("turned", "turned_hi", "turned_lo", "down_summed"))
        row_ready, row_hi_ready, row_lo_ready = sem("row_ready"), sem("row_hi_ready"), sem("row_lo_ready")
        gathered, even_out, odd_out, stored = sem("gathered"), sem("even_out"), sem("odd_out"), sem("stored")

        def pair_wait(eng, semaphore, pair, per_pair, at_first):
            if isinstance(pair, int) and pair == 0 and at_first <= 0:
                return
            eng.wait_ge(semaphore, pair * per_pair + at_first)

        def buffer_free(eng, summed, pair, s, first_use, at_first_use):
            if isinstance(pair, int) and pair == 0 and s < 2:
                eng.wait_ge(first_use, at_first_use)
            else:
                pair_wait(eng, summed, pair, SPP, s - 1)

        def over_pairs(eng, steps):
            steps(0)
            with eng.Fori(1, PAIRS) as pair:
                steps(pair)

        block = ctx.enter_context(nc.Block())

        @block.sync
        def _(sp):
            sp.dma_start(ids_sb[:], ids).then_inc(ids_in, 16)
            sp.dma_start(cols_sb[:], cols).then_inc(cols_in, 16)
            sp.dma_start(embT_sb, embT).then_inc(embT_in, 16)
            for c in range(DC):
                sp.dma_start(proj_sb[:, c], projT[:, c]).then_inc(proj_in[c], 16)
            for part, (dst, landed) in enumerate(((wq, wq_in), (wk, wk_in), (wv[:], wv_in))):
                sp.dma_start(dst, wqkvT[part]).then_inc(landed, 16)
                if part == 0:
                    sp.dma_start(emb_sb, emb).then_inc(emb_in, 16)
            sp.dma_start(wo[:], woT).then_inc(wo_in, 16)
            sp.dma_start(rows_sb[:], rows.to_broadcast([P, rows.shape[1]])).then_inc(rows_in, 16)

            def load_pair(pair):
                for s in range(SPP):
                    a, b = GROUP[s]
                    if isinstance(pair, int) and pair == 0:
                        if s == 2:
                            sp.wait_ge(wqkv_lo_done, DC)
                            sp.wait_ge(embT_scaled, 1)
                        if s == 3:
                            sp.wait_ge(projected, 1)
                            sp.wait_ge(emb_squared, 1)
                    pair_wait(sp, gu_hi_done, pair, SPP * DC, (s + 1 - SPP) * DC)
                    pair_wait(sp, gu_lo_done, pair, SPP * DC, (s + 1 - SPP) * DC)
                    sp.dma_start(raw_gu[:, s, :], gate_up_rows[pair * SPP + s]).then_inc(gu_in[s], 16)
                    if isinstance(pair, int) and pair == 0 and s >= 2:
                        sp.wait_ge(wqkv_lo_done, 2 * DC)
                        sp.wait_ge(projected, 1)
                    pair_wait(sp, dn_hi_done, pair, SPP, s + 1 - SPP)
                    pair_wait(sp, dn_lo_done, pair, SPP, s + 1 - SPP)
                    sp.dma_start(raw_dn[:, a:b, :], down[pair, :, a:b, :]).then_inc(dn_in[s], 16)

            gate_up_rows = gate_up.rearrange("e h p c g n -> (e h) p (c g n)")
            over_pairs(sp, load_pair)

            out_rows = out.rearrange("(p j) d -> p j d", j=TB)
            for j in range(0, TB, 2):
                sp.wait_ge(even_out, j // 2 + 1)
                sp.wait_ge(odd_out, j // 2 + 1)
                sp.dma_start(out_rows[:, j:j + 2, :], out_sb[:, j:j + 2, :]).then_inc(stored, 16)
            sp.wait_ge(stored, 16 * (TB // 2))

        @block.gpsimd
        def _(pool):
            pool.memset(ident_b[:], 0.0).then_inc(zeroed, 1)
            pool.memset(ident[:], 0.0).then_inc(zeroed, 1)
            pool.wait_ge(zeroed, 2)
            for square, n in ((ident_b, TB), (ident, P)):
                pool.affine_select(out=square[:], in_=square[:], compare_op=ALU.not_equal, fill=1.0,
                                   base=0, pattern=[[-1, n]], channel_multiplier=1).then_inc(consts, 1)
            pool.iota(row_index[:], [[0, 1]], base=0, channel_multiplier=1,
                      allow_small_or_imprecise_dtypes=True).then_inc(consts, 1)
            pool.memset(exponent[:], -0.5).then_inc(consts, 1)
            pool.wait_ge(emb_squared, 1)
            pool.tensor_scalar(c0, sumsq, RMS_EPS / D, RMS_EPS * RMS_EPS, ALU.mult, ALU.add).then_inc(c0_ready, 1)
            pool.wait_ge(scale_step, 3)
            pool.wait_ge(consts, 4)
            pool.tensor_tensor(scales, u2, exponent[:], ALU.pow).then_inc(scales_ready, 1)
            pool.wait_ge(h_ready, 1)
            pool.wait_ge(rows_in, 16)
            pool.tensor_tensor(hb[:], h[:], rows_sb[:, BO:BO + D], ALU.add).then_inc(hb_ready, 1)

            def split_pair(pair):
                for s in range(SPP):
                    if not (isinstance(pair, int) and pair == 0 and s == 0):
                        down_lo(pair, s)

            def down_lo(pair, s):
                a, b = GROUP[s]
                buf = s % 2
                pool.wait_ge(dn_in[s], (pair + 1) * 16)
                pair_wait(pool, dn_hi_done, pair, SPP, s + 1)
                buffer_free(pool, down_summed, pair, s, qkv_done, 3)
                pool.tensor_tensor(dn_lo[:, buf, 0:b - a, :], raw_dn[:, a:b, :],
                                   dn_hi[:, buf, 0:b - a, :].bitcast(F32), ALU.subtract).then_inc(dn_lo_done, 1)

            pool.wait_ge(moments2, 2)
            pool.tensor_scalar(u3, mv2[:, 1:2], LN_EPS, float(D * D), ALU.add, ALU.mult).then_inc(moments2, 1)
            pool.wait_ge(moments2, 3)
            pool.tensor_tensor(k2, u3, exponent[:, 0:1], ALU.pow).then_inc(k2_ready, 1)
            down_lo(0, 0)
            over_pairs(pool, split_pair)

        @block.scalar
        def _(act):
            def gu_hi_chunk(pair, s, c):
                buf = s % 2
                if c == 0:
                    act.wait_ge(gu_in[s], (pair + 1) * 16)
                    buffer_free(act, gu_summed, pair, s, qkv_done, s + 1)
                act.activation(gu_hi[:, buf, c, :, 0:HALF], raw_gu[:, s, c * 2 * HALF:(c + 1) * 2 * HALF]
                               .rearrange("p (g n) -> p g n", g=2), ACT.Copy).then_inc(gu_hi_done, 1)

            def down_hi(pair, s):
                a, b = GROUP[s]
                act.wait_ge(dn_in[s], (pair + 1) * 16)
                buffer_free(act, down_summed, pair, s, qkv_done, 3)
                act.activation(dn_hi[:, s % 2, 0:b - a, :], raw_dn[:, a:b, :], ACT.Copy).then_inc(dn_hi_done, 1)

            def silu_of(pair, s):
                pair_wait(act, gu_summed, pair, SPP, s + 1)
                pair_wait(act, inter_done, pair, SPP, s - 1)
                act.activation(silu[:, s % 2], ps_gu[:, 2 * (s % 2), 0:HALF], ACT.Silu,
                               scale=k2).then_inc(silu_done, 1)

            def interT_hi_of(pair, s):
                a, b = GROUP[s]
                pair_wait(act, turned, pair, SPP, s + 1)
                pair_wait(act, down_summed, pair, SPP, s - 1)
                act.activation(interT_hi[:, s % 2, 0:b - a, :],
                               ps_t[:, s % 2, 0:(b - a) * P].rearrange("p (c v) -> p c v", v=P),
                               ACT.Copy).then_inc(turned_hi, 1)

            def qkv_hi(part, landed, chunks):
                act.wait_ge(landed, 16)
                for c in chunks:
                    act.activation(wqkv_hi[part][:, c], (wq, wk, wv)[part][:, c], ACT.Copy).then_inc(wqkv_hi_done, 1)

            def qkv_scaled(part):
                act.wait_ge(qkv_done, part + 1)
                act.activation(qkv[:, part], ps_gu[:, part], ACT.Copy, scale=k_x1).then_inc(qkv_ready, 1)

            qkv_hi(0, wq_in, range(DC))
            act.wait_ge(x1_turned, 1)
            act.activation(x1T_hi[:, :, :], ps_t[:, 0].rearrange("p (c v) -> p c v", v=P),
                           ACT.Copy).then_inc(x1T_hi_ready, 1)
            act.wait_ge(emb_in, 16)
            act.activation(hb[:], emb_sb, ACT.Square, accum_out=sumsq).then_inc(emb_squared, 1)
            qkv_hi(1, wk_in, range(DC))
            act.wait_ge(x1_ready, 1)
            act.wait_ge(scales_ready, 1)
            act.activation(h[:], ps_x[:], ACT.Copy, scale=s_h).then_inc(h_ready, 1)
            qkv_scaled(0)
            qkv_hi(2, wv_in, range(DC))
            qkv_scaled(1)
            act.activation(gu_hi[:, 0, :, 0, HALF:], gate_w, ACT.Copy).then_inc(gate_split, 1)
            qkv_scaled(2)
            gu_hi_chunk(0, 0, 0)
            act.wait_ge(softmax_step, 2)
            act.activation(prob[:], score[:], ACT.Exp, bias=nmax).then_inc(exp_ready, 1)
            for c in range(1, DC):
                gu_hi_chunk(0, 0, c)
            act.wait_ge(prob_turned, 1)
            act.activation(probT[:], ps_t[:, 0, 0:P], ACT.Copy).then_inc(probT_ready, 1)
            for n in range(2):
                act.wait_ge(vo_done, n + 1)
                act.activation(vo[:, n * D // 2:(n + 1) * D // 2], vo_bank[n], ACT.Copy).then_inc(vo_ready, 1)
            down_hi(0, 0)
            act.wait_ge(x2_turned, 1)
            act.activation(x2T_hi[:, :, :], ps_t[:, 0].rearrange("p (c v) -> p c v", v=P),
                           ACT.Copy).then_inc(x2T_hi_ready, 1)
            for c in range(DC):
                gu_hi_chunk(0, 1, c)
            down_hi(0, 1)
            act.wait_ge(router_step, 2)
            act.activation(expd[:, 0:EXPERTS], logits[:, 0:EXPERTS], ACT.Exp, bias=lmax,
                           accum_out=lsum).then_inc(lexp_ready, 1)
            act.wait_ge(lexp_ready, 1)
            act.activation(spare, lsum, ACT.Silu).then_inc(silu_table, 1)

            def pair_steps(pair):
                for s in range(SPP):
                    first = isinstance(pair, int) and pair == 0
                    if not (first and s < 2):
                        silu_of(*before(pair, s, 2))
                    if not (first and s < 2):
                        gu_hi_chunk(pair, s, 0)
                    if not (first and s < 2):
                        interT_hi_of(*before(pair, s, 2))
                    if not (first and s < 2):
                        for c in range(1, DC):
                            gu_hi_chunk(pair, s, c)
                        if not (first and s == 2):
                            down_hi(*before(pair, s, 1))

            act.wait_ge(routed, 2)
            over_pairs(act, pair_steps)
            last = SPP - 1
            silu_of(PAIRS - 1, last - 1)
            interT_hi_of(PAIRS - 1, last - 1)
            down_hi(PAIRS - 1, last)
            silu_of(PAIRS - 1, last)
            interT_hi_of(PAIRS - 1, last)
            act.wait_ge(row_ready, 1)
            act.activation(row_hi, row[:], ACT.Copy).then_inc(row_hi_ready, 1)
            for j in range(0, TB, 2):
                act.wait_ge(gathered, j + 1)
                act.activation(out_sb[:, j, :], gather_bank[j % 8], ACT.Copy).then_inc(even_out, 1)

        @block.vector
        def _(dve):
            def gu_lo_chunk(pair, s, c):
                buf = s % 2
                if c == 0:
                    dve.wait_ge(gu_in[s], (pair + 1) * 16)
                    buffer_free(dve, gu_summed, pair, s, qkv_done, s + 1)
                pair_wait(dve, gu_hi_done, pair, SPP * DC, s * DC + c + 1)
                dve.tensor_tensor(gu_lo[:, buf, c, :, 0:HALF], raw_gu[:, s, c * 2 * HALF:(c + 1) * 2 * HALF]
                                  .rearrange("p (g n) -> p g n", g=2),
                                  gu_hi[:, buf, c, :, 0:HALF].bitcast(F32), ALU.subtract).then_inc(gu_lo_done, 1)

            def inter_of(pair, s):
                if isinstance(pair, int):
                    e = pair * 2 + s // HALVES
                    weight = comb[:, e:e + 1]
                else:
                    weight = comb[:, bass.ds(pair * 2 + s // HALVES, 1)]
                pair_wait(dve, silu_done, pair, SPP, s + 1)
                pair_wait(dve, turned, pair, SPP, s - 2)
                dve.scalar_tensor_tensor(out=inter[:, s * HALF:(s + 1) * HALF], in0=silu[:, s % 2], scalar=weight,
                                         in1=ps_gu[:, 2 * (s % 2) + 1, 0:HALF], op0=ALU.mult,
                                         op1=ALU.mult).then_inc(inter_done, 1)

            def interT_lo_of(pair, s):
                a, b = GROUP[s]
                pair_wait(dve, turned_hi, pair, SPP, s + 1)
                pair_wait(dve, down_summed, pair, SPP, s - 1)
                dve.tensor_tensor(interT_lo[:, s % 2, 0:b - a, :],
                                  ps_t[:, s % 2, 0:(b - a) * P].rearrange("p (c v) -> p c v", v=P),
                                  interT_hi[:, s % 2, 0:b - a, :].bitcast(F32), ALU.subtract).then_inc(turned_lo, 1)

            dve.memset(zeros[:], 0.0).then_inc(zeros_ready, 1)
            dve.wait_ge(ids_in, 16)
            dve.tensor_scalar(ids_f[:, 0], ids_sb[:], 0.0, float(P), ALU.is_lt, ALU.mult).then_inc(ids_fixed, 1)
            dve.wait_ge(ids_fixed, 1)
            dve.tensor_tensor(ids_f[:, 1], ids_f[:, 0], ids_sb[:], ALU.add).then_inc(ids_fixed, 1)
            dve.wait_ge(ids_fixed, 2)
            dve.tensor_scalar(ids_b[:], ids_f[:, 1], 0.0, float(P - 1), ALU.max, ALU.min).then_inc(ids_fixed, 1)
            dve.wait_ge(embT_in, 16)
            dve.wait_ge(cols_in, 16)
            dve.tensor_tensor(embT_w, embT_sb, cols_sb[:, NW:NW + DC, None].to_broadcast([P, DC, P]),
                              ALU.mult).then_inc(embT_scaled, 1)
            dve.wait_ge(consts, 4)
            for b in range(DC):
                dve.wait_ge(ids_spread, b + 1)
                dve.tensor_scalar(onehot[:, b * BANK:(b + 1) * BANK], ps_gu[:, b], row_index[:], 0.0,
                                  ALU.is_equal, ALU.add, accum_out=counts[:, b:b + 1]).then_inc(onehot_ready, 1)
            dve.wait_ge(projected, 1)
            dve.bn_stats(bn, ps_x[:]).then_inc(moments, 1)
            dve.wait_ge(moments, 1)
            dve.bn_aggr(mv, bn).then_inc(moments, 1)
            dve.wait_ge(moments, 2)
            dve.tensor_scalar(x1[:], ps_x[:], mean, None, ALU.subtract).then_inc(x1_ready, 1)
            dve.wait_ge(onehot_ready, 4)
            dve.tensor_reduce(count[:], counts[:], AX.X, ALU.add).then_inc(counted, 1)
            dve.wait_ge(counted, 1)
            dve.tensor_copy(count_wide[:], count[:, 0:1].to_broadcast([P, P])).then_inc(count_widened, 1)

            def qkv_lo(part, landed, chunks):
                dve.wait_ge(landed, 16)
                for c in chunks:
                    dve.wait_ge(wqkv_hi_done, part * DC + c + 1)
                    dve.tensor_tensor(wqkv_lo[part][:, c], (wq, wk, wv)[part][:, c],
                                      wqkv_hi[part][:, c].bitcast(F32), ALU.subtract).then_inc(wqkv_lo_done, 1)

            def add_bias(part, src, turned_part, ready):
                dve.wait_ge(turned_part, 1)
                bias = cols_sb[:, BQKV + part * DC:BQKV + (part + 1) * DC, None].to_broadcast([P, DC, P])
                dve.tensor_tensor(qkvT[:, part], src.rearrange("p (c v) -> p c v", v=P), bias,
                                  ALU.add).then_inc(ready, 1)

            qkv_lo(0, wq_in, range(2))
            dve.wait_ge(x1T_hi_ready, 1)
            dve.tensor_tensor(x1T_lo[:, :, :], ps_t[:, 0].rearrange("p (c v) -> p c v", v=P),
                              x1T_hi[:, :, :].bitcast(F32), ALU.subtract).then_inc(x1T_lo_ready, 1)
            qkv_lo(0, wq_in, range(2, DC))
            dve.wait_ge(c0_ready, 1)
            dve.tensor_tensor(v0, var, c0, ALU.add).then_inc(scale_step, 1)
            dve.wait_ge(scale_step, 1)
            dve.tensor_scalar(u2[:, 0:1], mean, mean, v0, ALU.mult, ALU.add).then_inc(scale_step, 1)
            dve.wait_ge(scale_step, 2)
            dve.tensor_scalar(u2[:, 1:2], u2[:, 0:1], LN_EPS, var, ALU.mult, ALU.add).then_inc(scale_step, 1)
            qkv_lo(1, wk_in, range(DC))
            dve.wait_ge(count_spread, 1)
            dve.tensor_copy(count_row[:], ps_t[:, 1, 0:P]).then_inc(counts_ready, 1)
            dve.tensor_scalar(absent_row[:], ps_t[:, 1, 0:P], 0.0, ABSENT, ALU.is_equal,
                              ALU.mult).then_inc(counts_ready, 1)
            add_bias(0, ps_gu[:, 0], q_turned, q_ready)
            qkv_lo(2, wv_in, range(DC))
            add_bias(1, ps_gu[:, 1], k_turned, k_ready)
            dve.wait_ge(gate_split, 1)
            dve.tensor_tensor(gu_lo[:, 0, :, 0, HALF:], gate_w, gu_hi[:, 0, :, 0, HALF:].bitcast(F32),
                              ALU.subtract).then_inc(gate_split, 1)
            add_bias(2, ps_gu[:, 2], v_turned, v_ready)
            dve.wait_ge(scored, 1)
            dve.wait_ge(counts_ready, 2)
            dve.scalar_tensor_tensor(out=score[:], in0=ps_t[:, 1, 0:P], scalar=SCALE, in1=absent_row[:],
                                     op0=ALU.mult, op1=ALU.add).then_inc(softmax_step, 1)
            dve.wait_ge(softmax_step, 1)
            dve.tensor_reduce(nmax, score[:], AX.X, ALU.max, negate=True).then_inc(softmax_step, 1)
            dve.wait_ge(exp_ready, 1)
            dve.scalar_tensor_tensor(out=score[:], in0=prob[:], scalar=1.0, in1=count_row[:], op0=ALU.mult,
                                     op1=ALU.mult, accum_out=rsum).then_inc(prob_ready, 1)
            dve.wait_ge(prob_ready, 1)
            dve.reciprocal(rinv, rsum).then_inc(softmax_step, 1)
            for c in range(DC):
                gu_lo_chunk(0, 0, c)
            dve.wait_ge(attended, 1)
            dve.wait_ge(softmax_step, 3)
            dve.wait_ge(hb_ready, 1)
            dve.scalar_tensor_tensor(out=h2[:], in0=ps_x[:], scalar=rinv, in1=hb[:], op0=ALU.mult,
                                     op1=ALU.add, accum_out=h2_sum).then_inc(h2_ready, 1)
            dve.wait_ge(h2_ready, 1)
            dve.tensor_scalar(x2[:], h2[:], float(D), h2_sum, ALU.mult, ALU.subtract).then_inc(x2_ready, 1)
            dve.bn_stats(bn2, h2[:]).then_inc(moments2, 1)
            dve.wait_ge(moments2, 1)
            dve.bn_aggr(mv2, bn2).then_inc(moments2, 1)
            dve.wait_ge(x2T_hi_ready, 1)
            dve.tensor_tensor(x2T_lo[:, :, :], ps_t[:, 0].rearrange("p (c v) -> p c v", v=P),
                              x2T_hi[:, :, :].bitcast(F32), ALU.subtract).then_inc(x2T_lo_ready, 1)
            for c in range(DC):
                gu_lo_chunk(0, 1, c)
            dve.memset(routing, NO_EXPERT).then_inc(router_step, 1)
            dve.wait_ge(routed, 1)
            dve.wait_ge(k2_ready, 1)
            dve.scalar_tensor_tensor(out=logits[:, 0:EXPERTS], in0=ps_gu[:, 0, HALF:HALF + EXPERTS], scalar=k2,
                                     in1=rows_sb[:, GB:GB + EXPERTS], op0=ALU.mult, op1=ALU.add).then_inc(routed, 1)
            dve.wait_ge(routed, 2)
            dve.tensor_reduce(lmax, logits[:, 0:EXPERTS], AX.X, ALU.max, negate=True).then_inc(router_step, 1)
            dve.wait_ge(lexp_ready, 1)
            dve.reciprocal(linv, lsum).then_inc(router_step, 1)
            dve.wait_ge(router_step, 3)
            dve.scalar_tensor_tensor(out=routing[:, 0:EXPERTS], in0=expd[:, 0:EXPERTS], scalar=linv,
                                     in1=rows_sb[:, EB:EB + EXPERTS], op0=ALU.mult,
                                     op1=ALU.add).then_inc(router_step, 1)
            dve.wait_ge(router_step, 4)
            dve.max(top[:, 0:8], routing).then_inc(router_step, 1)
            dve.wait_ge(router_step, 5)
            dve.memset(top[:, 2:8], NO_EXPERT).then_inc(router_step, 1)
            dve.wait_ge(router_step, 6)
            dve.match_replace(marked, top[:, 0:8], routing, TAKEN).then_inc(router_step, 1)
            dve.wait_ge(router_step, 7)
            dve.scalar_tensor_tensor(out=expd[:, 0:EXPERTS], in0=marked[:, 0:EXPERTS], scalar=TAKEN / 2,
                                     in1=routing[:, 0:EXPERTS], op0=ALU.is_lt, op1=ALU.mult).then_inc(router_step, 1)
            dve.wait_ge(router_step, 8)
            dve.tensor_scalar(comb[:, 0:EXPERTS], expd[:, 0:EXPERTS], k2, None, ALU.mult).then_inc(router_step, 1)
            dve.wait_ge(router_step, 9)

            def pair_steps(pair):
                for s in range(SPP):
                    first = isinstance(pair, int) and pair == 0
                    if not (first and s < 2):
                        inter_of(*before(pair, s, 2))
                    if not (first and s < 2):
                        gu_lo_chunk(pair, s, 0)
                    if not (first and s < 2):
                        interT_lo_of(*before(pair, s, 2))
                    if not (first and s < 2):
                        for c in range(1, DC):
                            gu_lo_chunk(pair, s, c)

            over_pairs(dve, pair_steps)
            last = SPP - 1
            inter_of(PAIRS - 1, last - 1)
            interT_lo_of(PAIRS - 1, last - 1)
            inter_of(PAIRS - 1, last)
            interT_lo_of(PAIRS - 1, last)
            dve.wait_ge(down_summed, STEPS)
            dve.tensor_tensor(row[:], ps_acc[:], h2[:], ALU.add).then_inc(row_ready, 1)
            dve.wait_ge(row_hi_ready, 1)
            dve.tensor_tensor(row_lo, row[:], row_hi.bitcast(F32), ALU.subtract).then_inc(row_lo_ready, 1)
            for j in range(1, TB, 2):
                dve.wait_ge(gathered, j + 1)
                dve.tensor_copy(out_sb[:, j, :], gather_bank[j % 8]).then_inc(odd_out, 1)

        @block.tensor
        def _(pe):
            def turn(dst, src, done):
                for c in range(DC):
                    ins = pe.transpose(dst[:, c * P:(c + 1) * P], src[:, c * P:(c + 1) * P], ident[:])
                ins.then_inc(done, 1)

            def keep_busy(products):
                for n in range(products):
                    pe.matmul(ps_acc[:], zeros[:].to_broadcast([P, P]), zeros[:].to_broadcast([P, BANK]),
                              start=True, stop=True)

            pe.wait_ge(zeros_ready, 1)
            keep_busy(WARM_UP)
            pe.wait_ge(ids_fixed, 3)
            pe.wait_ge(consts, 1)
            for c in range(DC):
                for j in range(c * TB // DC, (c + 1) * TB // DC):
                    ins = pe.matmul(ps_gu[:, j // 4, (j % 4) * P:(j % 4 + 1) * P],
                                    ident_b[:, j:j + 1].to_broadcast([TB, P]), ids_b[:], start=True, stop=True)
                ins.then_inc(ids_spread, 1)
                if c == 0:
                    pe.wait_ge(embT_scaled, 1)
                pe.wait_ge(proj_in[c], 16)
                ins = pe.matmul(ps_x[:], embT_w[:, c], proj_sb[:, c], start=(c == 0), stop=(c == DC - 1))
            ins.then_inc(projected, 1)
            keep_busy(8)
            pe.wait_ge(x1_ready, 1)
            pe.wait_ge(consts, 2)
            turn(ps_t[:, 0], x1[:], x1_turned)
            keep_busy(3)
            pe.wait_ge(x1T_hi_ready, 1)
            pe.wait_ge(onehot_ready, 4)

            def project(part, between=None):
                for n, (x, w) in enumerate(((x1T_hi, wqkv_hi), (x1T_lo, wqkv_hi), (x1T_hi, wqkv_lo))):
                    if n == 1:
                        pe.wait_ge(x1T_lo_ready, 1)
                    if n == 2 and between:
                        between()
                    for c in range(DC):
                        pe.wait_ge((wqkv_hi_done, wqkv_hi_done, wqkv_lo_done)[n], part * DC + c + 1)
                        ins = pe.matmul(ps_gu[:, part], x[:, c], w[part][:, c], start=(n == 0 and c == 0),
                                        stop=(n == 2 and c == DC - 1))
                ins.then_inc(qkv_done, 1)

            def turn_part(part, done):
                pe.wait_ge(qkv_ready, part + 1)
                turn(ps_gu[:, part], qkv[:, part], done)

            project(0)
            pe.wait_ge(count_widened, 1)
            pe.matmul(ps_t[:, 1, 0:P], count_wide[:], ident[:], start=True, stop=True).then_inc(count_spread, 1)
            project(1, between=lambda: turn_part(0, q_turned))
            project(2, between=lambda: turn_part(1, k_turned))
            pe.wait_ge(q_ready, 1)
            pe.wait_ge(k_ready, 1)
            pe.wait_ge(counts_ready, 2)
            for c in range(DC):
                ins = pe.matmul(ps_t[:, 1, 0:P], qkvT[:, 0, c], qkvT[:, 1, c], start=(c == 0), stop=(c == DC - 1))
            ins.then_inc(scored, 1)
            turn_part(2, v_turned)
            pe.wait_ge(wo_in, 16)
            pe.wait_ge(v_ready, 1)
            for n in range(2):
                for c in range(DC):
                    ins = pe.matmul(vo_bank[n], qkvT[:, 2, c], wo[:, c, n * D // 2:(n + 1) * D // 2],
                                    start=(c == 0), stop=(c == DC - 1))
                ins.then_inc(vo_done, 1)
                if n == 0:
                    pe.wait_ge(prob_ready, 1)
                    pe.transpose(ps_t[:, 0, 0:P], score[:], ident[:]).then_inc(prob_turned, 1)
            pe.wait_ge(probT_ready, 1)
            pe.wait_ge(h_ready, 1)
            for n in range(2):
                pe.wait_ge(vo_ready, n + 1)
                ins = pe.matmul(ps_x[:, n * D // 2:(n + 1) * D // 2], probT[:], vo[:, n * D // 2:(n + 1) * D // 2],
                                start=True, stop=True)
            ins.then_inc(attended, 1)
            keep_busy(7)
            pe.wait_ge(x2_ready, 1)
            turn(ps_t[:, 0], x2, x2_turned)
            keep_busy(7)

            def gate_up_sum(pair, s, chunks):
                buf = s % 2
                if 0 in chunks:
                    pair_wait(pe, silu_done, pair, SPP, s - 1)
                    pair_wait(pe, inter_done, pair, SPP, s - 1)
                order = [(c, g) for c in chunks for g in range(2)]
                if isinstance(pair, int) and pair == s == 0:
                    order.sort(key=lambda cg: cg[1])
                for c, g in order:
                    pair_wait(pe, gu_hi_done, pair, SPP * DC, s * DC + c + 1)
                    pair_wait(pe, gu_lo_done, pair, SPP * DC, s * DC + c + 1)
                    n_cols = HALF + EXPERTS * (isinstance(pair, int) and pair == s == g == 0)
                    for n, (x, w) in enumerate(((x2T_hi, gu_hi), (x2T_hi, gu_lo), (x2T_lo, gu_hi))):
                        ins = pe.matmul(ps_gu[:, 2 * buf + g, 0:n_cols], x[:, c], w[:, buf, c, g, 0:n_cols],
                                        start=(c == 0 and n == 0), stop=(c == DC - 1 and n == 2))
                    if c == DC - 1 and g == 0 and isinstance(pair, int) and pair == s == 0:
                        ins.then_inc(routed, 1)
                if DC - 1 in chunks:
                    ins.then_inc(gu_summed, 1)

            def turn_inter(pair, s):
                a, b = GROUP[s]
                pair_wait(pe, inter_done, pair, SPP, s + 1)
                pair_wait(pe, turned_lo, pair, SPP, s - 1)
                for c in range(a, b):
                    ins = pe.transpose(ps_t[:, s % 2, (c - a) * P:(c - a + 1) * P],
                                       inter[:, c * P:(c + 1) * P], ident[:])
                ins.then_inc(turned, 1)

            def down_sum(pair, s, first=False, last=False):
                a, b = GROUP[s]
                buf = s % 2
                pair_wait(pe, turned_hi, pair, SPP, s + 1)
                for n, (x, w) in enumerate(((interT_hi, dn_hi), (interT_hi, dn_lo), (interT_lo, dn_hi))):
                    pair_wait(pe, (dn_hi_done, dn_lo_done, turned_lo)[n], pair, SPP, s + 1)
                    for c in range(b - a):
                        ins = pe.matmul(ps_acc[:], x[:, buf, c], w[:, buf, c], start=(first and c == 0 and n == 0),
                                        stop=(last and c == b - a - 1 and n == 2))
                ins.then_inc(down_summed, 1)

            pe.wait_ge(x2T_hi_ready, 1)
            pe.wait_ge(x2T_lo_ready, 1)
            pe.wait_ge(gate_split, 2)
            pe.wait_ge(v_ready, 1)
            pe.wait_ge(vo_ready, 2)

            def pair_steps(pair):
                for s in range(SPP):
                    first = isinstance(pair, int) and pair == 0
                    cut = DC if first and s == 0 else DC - 1 if first and s == 1 else DC // 2
                    gate_up_sum(pair, s, range(cut))
                    if not (first and s == 0):
                        turn_inter(*before(pair, s, 1))
                        gate_up_sum(pair, s, range(cut, DC))
                    if not (first and s == 0):
                        down_sum(*before(pair, s, 1), first=(first and s == 1))

            over_pairs(pe, pair_steps)
            turn_inter(PAIRS - 1, SPP - 1)
            down_sum(PAIRS - 1, SPP - 1, last=True)
            for j in range(TB):
                if j == 0:
                    pe.wait_ge(row_hi_ready, 1)
                if j >= 8:
                    pe.wait_ge(even_out if j % 2 == 0 else odd_out, j // 2 - 3)
                pe.matmul(gather_bank[j % 8], onehot[:, j * P:(j + 1) * P], row_hi, start=True, stop=False)
                if j == 0:
                    pe.wait_ge(row_lo_ready, 1)
                pe.matmul(gather_bank[j % 8], onehot[:, j * P:(j + 1) * P], row_lo, start=False,
                          stop=True).then_inc(gathered, 1)


def before(pair, s, n, steps=4):
    return (pair, s - n) if s >= n else (pair - 1, s - n + steps)


def kernel(**inputs):
    import numpy as np
    import concourse.bacc as bacc
    from concourse.bass_utils import run_bass_kernel_spmd

    a = {k: np.asarray(v) for k, v in inputs.items()}
    x, emb = a["x"], a["L0_tok_emb_table"]
    T, D = x.shape[1], emb.shape[1]
    DC, TB = D // P, T // P
    w_gu, w_dn = a["L0_ffn_w_gate_up"], a["L0_ffn_w_down"]
    E, I = w_gu.shape[0], w_dn.shape[2]
    H = 2
    half = I // H

    def chunked(m):
        return m.reshape(DC, P, m.shape[1]).transpose(1, 0, 2)

    def column(v):
        return v.reshape(-1, P).T

    data = {
        "ids": x.reshape(P, TB).T,
        "emb": emb,
        "embT": chunked(emb.T),
        "cols": np.concatenate([column(a["L0_tok_norm_weight"]), column(a["L0_attn_b_qkv"]),
                                chunked(a["L0_ffn_gate_w"].T).reshape(P, DC * E)], axis=1),
        "rows": np.concatenate([a["L0_attn_b_out"], a["L0_ffn_gate_b"], a["L0_ffn_expert_bias"]])[None, :],
        "projT": chunked(a["L0_tok_proj_weight"].T),
        "wqkvT": np.stack([chunked(w.T) for w in np.split(a["L0_attn_w_qkv"], 3)]),
        "woT": chunked(a["L0_attn_w_out"].T),
        "gate_up": w_gu.reshape(E, 2, H, half, DC, P).transpose(0, 2, 5, 4, 1, 3),
        "down": w_dn.transpose(0, 2, 1).reshape(E // 2, 2 * I // P, P, D).transpose(0, 2, 1, 3),
    }
    data = {k: np.ascontiguousarray(v) for k, v in data.items()}
    nc = bacc.Bacc("TRN2", target_bir_lowering=False, num_devices=1)
    aps = [nc.dram_tensor(k, v.shape, mybir.dt.from_np(v.dtype), kind="ExternalInput").ap() for k, v in data.items()]
    out = nc.dram_tensor("out", (T, D), F32, kind="ExternalOutput").ap()
    tower_program(nc, *aps, out)
    result = run_bass_kernel_spmd(nc, [data], core_ids=[0])
    return result.results[0]["out"].reshape(1, T, D)
```

```python
from contextlib import ExitStack

import concourse.bass as bass
from concourse import mybir

F32 = mybir.dt.float32
F32R = mybir.dt.float32r
I32 = mybir.dt.int32
BF16 = mybir.dt.bfloat16
ALU = mybir.AluOpType
ACT = mybir.ActivationFunctionType
AX = mybir.AxisListType

P = 128
BANK = 512
RMS_EPS = 1e-6
LN_EPS = 1e-5
ABSENT = -1e30
NO_EXPERT = -3e38
TAKEN = -1e38
WARM_UP = 6


def tower_program(nc, ids, embT, cols, rows, projT, wqkvT, woT, gate_up, down, out):
    T = out.shape[0]
    DC = embT.shape[1]
    D = DC * P
    TB = T // P
    EXPERTS, HALVES, _, _, _, HALF = gate_up.shape
    STEPS = EXPERTS * HALVES
    SPP = 2 * HALVES
    PAIRS = STEPS // SPP
    CHUNKS = SPP * HALF // P
    EDGE = [(s * HALF) // P for s in range(SPP + 1)]
    GROUP = [(EDGE[s], EDGE[s + 1]) for s in range(SPP)]
    GMAX = max(b - a for a, b in GROUP)
    GU = DC * 2 * HALF
    SCALE = float(D) ** -0.5
    assert embT.shape[2] == P and T % P == 0 and HALF * SPP == CHUNKS * P and D == BANK and T == DC * BANK
    NW, BQKV, GW = 0, DC, DC + 3 * DC
    BO, GB, EB = 0, D, D + EXPERTS

    with ExitStack() as ctx:
        def sb(name, shape, dt=F32):
            return ctx.enter_context(nc.sbuf_tensor(name, shape, dt))

        def sem(name):
            return ctx.enter_context(nc.semaphore(name))

        raw_gu = sb("raw_gu", [P, SPP, GU])
        raw_dn = sb("raw_dn", [P, CHUNKS, D])
        gu_hi = sb("gu_hi", [P, 2, DC, 2, HALF + EXPERTS], F32R)
        gu_lo = sb("gu_lo", [P, 2, DC, 2, HALF + EXPERTS], F32R)
        dn_hi = sb("dn_hi", [P, 2, GMAX, D], F32R)
        dn_lo = sb("dn_lo", [P, 2, GMAX, D], F32R)
        onehot = sb("onehot", [P, T], F32R)
        wk = sb("wk", [P, DC, D])
        wo = sb("wo", [P, DC, D])
        ident_b = sb("ident_b", [P, TB], BF16)
        zeros = sb("zeros", [P, 1], BF16)
        wv = raw_gu[:, 2, 0:DC * D].rearrange("p (c o) -> p c o", c=DC)
        embT_sb = raw_gu[:, 2, DC * D:DC * D + DC * P].rearrange("p (c v) -> p c v", c=DC)
        proj_sb = raw_gu[:, 3, 0:DC * D].rearrange("p (c o) -> p c o", c=DC)
        row_sb = raw_gu[0:1, 1, 0:rows.shape[1]]
        late = raw_dn[:, GROUP[2][0]:, :].rearrange("p c d -> p (c d)")
        wq = late[:, 0:DC * D].rearrange("p (c o) -> p c o", c=DC)
        embT_w = late[:, DC * D:DC * D + DC * P].rearrange("p (c v) -> p c v", c=DC)
        BUF = DC * 2 * (HALF + EXPERTS)
        flat = "p a c g n -> p (a c g n)"
        wqkv_hi, wqkv_lo = (
            [gu.rearrange(flat)[:, 0:DC * D], gu.rearrange(flat)[:, BUF:BUF + DC * D],
             dn.rearrange("p a c d -> p (a c d)")[:, 0:DC * D]]
            for gu, dn in ((gu_hi[:, :, :, :, :], dn_hi[:, :, :, :]), (gu_lo[:, :, :, :, :], dn_lo[:, :, :, :])))
        wqkv_hi, wqkv_lo = ([w.rearrange("p (c o) -> p c o", c=DC) for w in parts] for parts in (wqkv_hi, wqkv_lo))
        assert BUF >= GMAX * (D + P)
        last_dn_hi, last_dn_lo = (
            gu.rearrange(flat)[:, 0:GMAX * D].rearrange("p (c o) -> p c o", c=GMAX)
            for gu in (gu_hi[:, :, :, :, :], gu_lo[:, :, :, :, :]))
        last_interT_hi, last_interT_lo = (
            gu.rearrange(flat)[:, GMAX * D:GMAX * (D + P)].rearrange("p (c v) -> p c v", c=GMAX)
            for gu in (gu_hi[:, :, :, :, :], gu_lo[:, :, :, :, :]))
        out_sb = raw_gu[:, :, :].rearrange("p s n -> p (s n)")[:, 0:TB * D].rearrange("p (j d) -> p j d", j=TB)

        cols_sb = sb("cols_sb", [P, cols.shape[1]])
        gate_w = cols_sb[:, GW:GW + DC * EXPERTS].rearrange("p (c e) -> p c e", c=DC)
        rows_sb = sb("rows_sb", [P, rows.shape[1]])
        ones = sb("ones", [P, 1])
        ids_sb = sb("ids_sb", [TB, P], I32)
        ids_f = sb("ids_f", [TB, 2, P])
        ids_b = sb("ids_b", [P, P], BF16)
        ident = sb("ident", [P, P])
        ident_r = sb("ident_r", [P, P], F32R)
        row_index = sb("row_index", [P, 1])
        exponent = sb("exponent", [P, 2])
        counts = sb("counts", [P, DC])
        count = sb("count", [P, 1])
        count_wide = sb("count_wide", [P, P])
        count_row = sb("count_row", [P, P])
        absent_row = sb("absent_row", [P, P])
        stat = sb("stat", [P, 64])
        h = sb("h", [P, D])
        hb = sb("hb", [P, D])
        embT_sq = hb[:].rearrange("p (c v) -> p c v", c=DC)
        x1 = sb("x1", [P, D])
        qkv = sb("qkv", [P, 3, D])
        x1T_hi = sb("x1T_hi", [P, DC, P], F32R)
        x1T_lo = sb("x1T_lo", [P, DC, P], F32R)
        qkvT = sb("qkvT", [P, 3, DC, P])
        vo = sb("vo", [P, D])
        score = sb("score", [P, P])
        prob = sb("prob", [P, P])
        probT = sb("probT", [P, P])
        h2 = sb("h2", [P, D])
        x2T_hi, x2T_lo = x1T_hi, x1T_lo
        router = sb("router", [P, 8, 16])
        silu = sb("silu", [P, 2, HALF])
        interT_hi = sb("interT_hi", [P, 2, GMAX, P], F32R)
        interT_lo = sb("interT_lo", [P, 2, GMAX, P], F32R)
        x2 = x1
        inter = qkvT[:, :, :, :].rearrange("p a c v -> p (a c v)")[:, 0:SPP * HALF]
        h2_hi, h2_lo = (t[:, :, :, :].rearrange("p a c v -> p (a c v)")[:, 0:D] for t in (interT_hi, interT_lo))
        right = h[:, D // 2:D]
        row_hi, row_lo = (t[:, :, :].rearrange("p c v -> p (c v)") for t in (x2T_hi, x2T_lo))

        def st(i, n=1):
            return stat[:, i:i + n]

        c0, bn, mv, v0, u2, scales, nmax, rsum, rinv = (
            st(1), st(2, 6), st(8, 2), st(10), st(12, 2), st(14, 2), st(16), st(17), st(18))
        bn2, mv2, u3, k2, lmax, lsum, linv = st(20, 6), st(26, 2), st(28), st(29), st(30), st(31), st(32)
        h2_sum, spare = st(33), st(34, 2)
        mean, var, s_h, k_x1 = mv[:, 0:1], mv[:, 1:2], scales[:, 0:1], scales[:, 1:2]
        logits, expd, routing, top, marked, comb = (router[:, i, :] for i in range(6))

        ps_gu = ctx.enter_context(nc.psum_tensor("ps_gu", [P, 4, BANK], F32))
        ps_t = ctx.enter_context(nc.psum_tensor("ps_t", [P, 2, BANK], F32))
        ps_x = ctx.enter_context(nc.psum_tensor("ps_x", [P, BANK], F32))
        ps_acc = ctx.enter_context(nc.psum_tensor("ps_acc", [P, BANK], F32))
        vo_bank = [ps_gu[:, 3, 0:D // 2], ps_acc[:, 0:D // 2]]
        gather_bank = [ps_gu[:, 0], ps_gu[:, 1], ps_gu[:, 2], ps_gu[:, 3], ps_t[:, 0], ps_t[:, 1]]
        GATHER_BANKS = len(gather_bank)
        HW = D // 2
        half_cols = [slice(0, HW), slice(HW, D)]
        GATHERS = ([(0, 0, 1), (0, 1, 1)] + [(0, j, 2) for j in range(2, TB, 2)]
                   + [(1, j, 2) for j in range(0, TB, 2)])
        STORES = [[0], [1], [2], [3], [4, 5], [6], [7], [8], [9], [10], [11, 12], [13, 14], [15, 16]]
        assert TB == 16

        ids_in, cols_in, rows_in, embT_in = (sem(n) for n in ("ids_in", "cols_in", "rows_in", "embT_in"))
        proj_in = [sem(f"proj_in{c}") for c in range(DC)]
        wv_in, wq_in, wk_in, wo_in = (sem(n) for n in ("wv_in", "wq_in", "wk_in", "wo_in"))
        gu_in = [sem(f"gu_in{s}") for s in range(SPP)]
        dn_in = [sem(f"dn_in{s}") for s in range(SPP)]
        zeroed, consts, zeros_ready = sem("zeroed"), sem("consts"), sem("zeros_ready")
        ids_fixed, ids_spread, onehot_ready = sem("ids_fixed"), sem("ids_spread"), sem("onehot_ready")
        counted, count_widened, count_spread, counts_ready = (
            sem(n) for n in ("counted", "count_widened", "count_spread", "counts_ready"))
        embT_squared, sumsq_done, embT_scaled, projected = (
            sem(n) for n in ("embT_squared", "sumsq_done", "embT_scaled", "projected"))
        rows_spread, rows_ready = sem("rows_spread"), sem("rows_ready")
        moments, c0_ready, scale_step, scales_ready = (
            sem(n) for n in ("moments", "c0_ready", "scale_step", "scales_ready"))
        x1_ready, h_ready, hb_ready, x1_turned, x1T_hi_ready, x1T_lo_ready = (
            sem(n) for n in ("x1_ready", "h_ready", "hb_ready", "x1_turned", "x1T_hi_ready", "x1T_lo_ready"))
        wqkv_hi_done, wqkv_lo_done = sem("wqkv_hi_done"), sem("wqkv_lo_done")
        wk_last_lo_done = sem("wk_last_lo_done")
        gate_split = sem("gate_split")
        qkv_done, qkv_ready, q_turned, k_turned, v_turned, q_ready, k_ready, v_ready = (
            sem(n) for n in ("qkv_done", "qkv_ready", "q_turned", "k_turned", "v_turned",
                             "q_ready", "k_ready", "v_ready"))
        scored, softmax_step, exp_ready, prob_ready = (
            sem(n) for n in ("scored", "softmax_step", "exp_ready", "prob_ready"))
        vo_done, vo_ready, prob_turned, probT_ready, attended = (
            sem(n) for n in ("vo_done", "vo_ready", "prob_turned", "probT_ready", "attended"))
        ident_ready, h2_hi_ready, h2_lo_ready = (
            sem(n) for n in ("ident_ready", "h2_hi_ready", "h2_lo_ready"))
        h2_ready, moments2, k2_ready, x2_ready, x2_turned, x2T_hi_ready, x2T_lo_ready = (
            sem(n) for n in ("h2_ready", "moments2", "k2_ready", "x2_ready", "x2_turned",
                             "x2T_hi_ready", "x2T_lo_ready"))
        routed, router_step, lexp_ready, silu_table = (
            sem(n) for n in ("routed", "router_step", "lexp_ready", "silu_table"))
        gu_hi_done, gu_lo_done = sem("gu_hi_done"), sem("gu_lo_done")
        dn_hi_done, dn_lo_done = sem("dn_hi_done"), sem("dn_lo_done")
        pool_lo_done = sem("pool_lo_done")
        last_lo_done = sem("last_lo_done")
        last_gate_summed = sem("last_gate_summed")
        gu_summed, silu_done, inter_done = sem("gu_summed"), sem("silu_done"), sem("inter_done")
        turned, turned_hi, turned_lo, down_summed = (
            sem(n) for n in ("turned", "turned_hi", "turned_lo", "down_summed"))
        row_hi_ready, row_lo_ready = sem("row_hi_ready"), sem("row_lo_ready")
        half_summed, right_joined = sem("half_summed"), sem("right_joined")
        gathered, even_out, odd_out, stored = sem("gathered"), sem("even_out"), sem("odd_out"), sem("stored")

        def gu_chunk(s, c):
            return raw_gu[:, s, c * 2 * HALF:(c + 1) * 2 * HALF].rearrange("p (g n) -> p g n", g=2)

        def pair_wait(eng, semaphore, pair, per_pair, at_first):
            if isinstance(pair, int) and pair == 0 and at_first <= 0:
                return
            eng.wait_ge(semaphore, pair * per_pair + at_first)

        def buffer_free(eng, summed, pair, s, first_use, at_first_use):
            if isinstance(pair, int) and pair == 0 and s < 2:
                eng.wait_ge(first_use, at_first_use)
            else:
                pair_wait(eng, summed, pair, SPP, s - 1)

        def is_last(pair, s):
            return isinstance(pair, int) and pair == PAIRS - 1 and s == SPP - 1

        def peel_both(eng, steps):
            steps(0)
            with eng.Fori(1, PAIRS - 1) as pair:
                steps(pair)
            steps(PAIRS - 1)

        def over_pairs(eng, steps):
            steps(0)
            with eng.Fori(1, PAIRS) as pair:
                steps(pair)

        def copy_out(eng, i, done):
            n, j, blocks = GATHERS[i]
            src = gather_bank[i % GATHER_BANKS][:, 0:blocks * HW].rearrange("p (j d) -> p j d", j=blocks)
            eng.wait_ge(gathered, i + 1)
            if done is even_out:
                eng.activation(out_sb[:, j:j + blocks, half_cols[n]], src, ACT.Copy).then_inc(done, 1)
            else:
                eng.tensor_copy(out_sb[:, j:j + blocks, half_cols[n]], src).then_inc(done, 1)

        block = ctx.enter_context(nc.Block())

        @block.sync
        def _(sp):
            sp.dma_start(ids_sb[:], ids).then_inc(ids_in, 16)
            sp.dma_start(cols_sb[:], cols).then_inc(cols_in, 16)
            for c in range(DC):
                sp.dma_start(proj_sb[:, c], projT[:, c]).then_inc(proj_in[c], 16)
            for part, (dst, landed) in enumerate(((wv, wv_in), (wq, wq_in), (wk[:], wk_in))):
                sp.dma_start(dst, wqkvT[part]).then_inc(landed, 16)
            sp.dma_start(wo[:], woT).then_inc(wo_in, 16)

            def load_pair(pair):
                for s in range(SPP):
                    a, b = GROUP[s]
                    if isinstance(pair, int) and pair == 0:
                        if s == 1:
                            sp.wait_ge(rows_spread, 1)
                        if s == 2:
                            sp.wait_ge(wqkv_lo_done, DC)
                            sp.wait_ge(embT_scaled, 1)
                            sp.wait_ge(embT_squared, 1)
                        if s == 3:
                            sp.wait_ge(projected, 1)
                    pair_wait(sp, gu_hi_done, pair, SPP * DC, (s + 1 - SPP) * DC)
                    pair_wait(sp, gu_lo_done, pair, SPP * DC, (s + 1 - SPP) * DC)
                    sp.dma_start(raw_gu[:, s, :], gate_up_rows[pair * SPP + s]).then_inc(gu_in[s], 16)
                    if isinstance(pair, int) and pair == 0 and s >= 2:
                        sp.wait_ge(wqkv_lo_done, 2 * DC)
                        sp.wait_ge(projected, 1)
                    pair_wait(sp, dn_hi_done, pair, SPP, s + 1 - SPP)
                    pair_wait(sp, dn_lo_done, pair, SPP, s + 1 - SPP)
                    sp.dma_start(raw_dn[:, a:b, :], down[pair, :, a:b, :]).then_inc(dn_in[s], 16)

            gate_up_rows = gate_up.rearrange("e h p c g n -> (e h) p (c g n)")
            over_pairs(sp, load_pair)

            out_rows = out.rearrange("(p j) d -> p j d", j=TB)
            for loads in STORES:
                if any(i % 2 == 0 for i in loads):
                    sp.wait_ge(even_out, loads[-1] // 2 + 1)
                if any(i % 2 == 1 for i in loads):
                    sp.wait_ge(odd_out, (loads[-1] + 1) // 2)
                n, a, _ = GATHERS[loads[0]]
                b = GATHERS[loads[-1]][1] + GATHERS[loads[-1]][2]
                sp.dma_start(out_rows[:, a:b, half_cols[n]], out_sb[:, a:b, half_cols[n]]).then_inc(stored, 16)
            sp.wait_ge(stored, 16 * len(STORES))

        @block.gpsimd
        def _(pool):
            pool.memset(ident_b[:], 0.0).then_inc(zeroed, 1)
            pool.memset(ident[:], 0.0).then_inc(zeroed, 1)
            pool.wait_ge(zeroed, 2)
            for square, n in ((ident_b, TB), (ident, P)):
                pool.affine_select(out=square[:], in_=square[:], compare_op=ALU.not_equal, fill=1.0,
                                   base=0, pattern=[[-1, n]], channel_multiplier=1).then_inc(consts, 1)
            pool.iota(row_index[:], [[0, 1]], base=0, channel_multiplier=1,
                      allow_small_or_imprecise_dtypes=True).then_inc(consts, 1)
            pool.memset(exponent[:], -0.5).then_inc(consts, 1)
            pool.memset(ones[:], 1.0).then_inc(consts, 1)
            pool.wait_ge(scale_step, 3)
            pool.wait_ge(consts, 4)
            pool.tensor_tensor(scales, u2, exponent[:], ALU.pow).then_inc(scales_ready, 1)
            pool.wait_ge(wqkv_hi_done, 3 * DC)
            pool.tensor_tensor(wqkv_lo[2][:, DC - 1], wk[:, DC - 1], wqkv_hi[2][:, DC - 1].bitcast(F32),
                               ALU.subtract).then_inc(wk_last_lo_done, 1)
            pool.wait_ge(h_ready, 1)
            pool.wait_ge(rows_ready, 1)
            pool.tensor_tensor(hb[:], h[:], rows_sb[:, BO:BO + D], ALU.add).then_inc(hb_ready, 1)

            def split_pair(pair):
                if not isinstance(pair, int):
                    down_lo(pair - 1, SPP - 1)
                for s in range(SPP - 1):
                    if not (isinstance(pair, int) and pair == 0 and s == 0):
                        down_lo(pair, s)

            def down_lo(pair, s):
                a, b = GROUP[s]
                buf = s % 2
                pool.wait_ge(dn_in[s], (pair + 1) * 16)
                pair_wait(pool, dn_hi_done, pair, SPP, s + 1)
                buffer_free(pool, down_summed, pair, s, qkv_done, 3)
                pool.tensor_tensor(dn_lo[:, buf, 0:b - a, :], raw_dn[:, a:b, :],
                                   dn_hi[:, buf, 0:b - a, :].bitcast(F32), ALU.subtract).then_inc(dn_lo_done, 1)

            pool.wait_ge(gu_hi_done, 1)
            pool.wait_ge(qkv_done, 1)
            pool.tensor_tensor(gu_lo[:, 0, 0, :, 0:HALF], gu_chunk(0, 0),
                               gu_hi[:, 0, 0, :, 0:HALF].bitcast(F32), ALU.subtract).then_inc(gu_lo_done, 1)
            pool.wait_ge(h2_hi_ready, 1)
            pool.tensor_tensor(h2_lo, h2[:], h2_hi.bitcast(F32), ALU.subtract).then_inc(h2_lo_ready, 1)
            pool.wait_ge(moments2, 2)
            pool.tensor_scalar(u3, mv2[:, 1:2], LN_EPS, float(D * D), ALU.add, ALU.mult).then_inc(moments2, 1)
            pool.wait_ge(moments2, 3)
            pool.tensor_tensor(k2, u3, exponent[:, 0:1], ALU.pow).then_inc(k2_ready, 1)
            pool.wait_ge(gu_hi_done, 2 * DC)
            pool.tensor_tensor(gu_lo[:, 1, DC - 1, :, 0:HALF], gu_chunk(1, DC - 1),
                               gu_hi[:, 1, DC - 1, :, 0:HALF].bitcast(F32), ALU.subtract).then_inc(pool_lo_done, 1)
            down_lo(0, 0)
            over_pairs(pool, split_pair)

        @block.scalar
        def _(act):
            act.dma_start(embT_sb, embT).then_inc(embT_in, 16)
            act.dma_start(row_sb, rows).then_inc(rows_in, 16)

            def gu_hi_chunk(pair, s, c):
                buf = s % 2
                if c == 0:
                    act.wait_ge(gu_in[s], (pair + 1) * 16)
                    buffer_free(act, gu_summed, pair, s, qkv_done, s + 1)
                act.activation(gu_hi[:, buf, c, :, 0:HALF], gu_chunk(s, c), ACT.Copy).then_inc(gu_hi_done, 1)

            def down_hi(pair, s):
                a, b = GROUP[s]
                act.wait_ge(dn_in[s], (pair + 1) * 16)
                buffer_free(act, down_summed, pair, s, qkv_done, 3)
                act.activation(dn_hi[:, s % 2, 0:b - a, :], raw_dn[:, a:b, :], ACT.Copy).then_inc(dn_hi_done, 1)

            def last_down_hi(c):
                act.wait_ge(dn_in[SPP - 1], PAIRS * 16)
                act.wait_ge(gu_summed, STEPS - 1)
                act.activation(last_dn_hi[:, c, :], raw_dn[:, GROUP[SPP - 1][0] + c, :], ACT.Copy).then_inc(
                    dn_hi_done, 1)

            def silu_of(pair, s):
                if is_last(pair, s):
                    act.wait_ge(last_gate_summed, 1)
                else:
                    pair_wait(act, gu_summed, pair, SPP, s + 1)
                pair_wait(act, inter_done, pair, SPP, s - 1)
                act.activation(silu[:, s % 2], ps_gu[:, 2 * (s % 2), 0:HALF], ACT.Silu,
                               scale=k2).then_inc(silu_done, 1)

            def interT_hi_of(pair, s):
                a, b = GROUP[s]
                pair_wait(act, turned, pair, SPP, s + 1)
                if is_last(pair, s):
                    dst = last_interT_hi[:, 0:b - a, :]
                else:
                    pair_wait(act, down_summed, pair, SPP, s - 1)
                    dst = interT_hi[:, s % 2, 0:b - a, :]
                act.activation(dst,
                               ps_t[:, s % 2, 0:(b - a) * P].rearrange("p (c v) -> p c v", v=P),
                               ACT.Copy).then_inc(turned_hi, 1)

            def qkv_hi(part, landed, chunks):
                act.wait_ge(landed, 16)
                for c in chunks:
                    act.activation(wqkv_hi[part][:, c], (wv, wq, wk)[part][:, c], ACT.Copy).then_inc(wqkv_hi_done, 1)

            def qkv_scaled(part):
                act.wait_ge(qkv_done, part + 1)
                act.activation(qkv[:, part], ps_gu[:, part], ACT.Copy, scale=k_x1).then_inc(qkv_ready, 1)

            act.wait_ge(embT_in, 16)
            act.activation(embT_sq, embT_sb, ACT.Square).then_inc(embT_squared, 1)
            act.wait_ge(consts, 2)
            act.activation(ident_r[:], ident[:], ACT.Copy).then_inc(ident_ready, 1)
            qkv_hi(0, wv_in, range(DC))
            act.wait_ge(x1_turned, 1)
            act.activation(x1T_hi[:, :, :], ps_t[:, 0].rearrange("p (c v) -> p c v", v=P),
                           ACT.Copy).then_inc(x1T_hi_ready, 1)
            act.wait_ge(rows_spread, 1)
            act.activation(rows_sb[:, 0:D], ps_acc[:], ACT.Copy).then_inc(rows_ready, 1)
            act.activation(rows_sb[:, D:], ps_gu[:, 3, 0:2 * EXPERTS], ACT.Copy).then_inc(rows_ready, 1)
            qkv_hi(1, wq_in, range(DC))
            act.wait_ge(scales_ready, 1)
            qkv_scaled(0)
            qkv_hi(2, wk_in, range(DC))
            act.wait_ge(x1_ready, 1)
            act.activation(h[:], ps_x[:], ACT.Copy, scale=s_h).then_inc(h_ready, 1)
            qkv_scaled(1)
            act.activation(gu_hi[:, 0, :, 0, HALF:], gate_w, ACT.Copy).then_inc(gate_split, 1)
            qkv_scaled(2)

            def vo_half(n):
                act.wait_ge(vo_done, n + 1)
                act.activation(vo[:, n * D // 2:(n + 1) * D // 2], vo_bank[n], ACT.Copy).then_inc(vo_ready, 1)

            gu_hi_chunk(0, 0, 0)
            vo_half(0)
            act.wait_ge(softmax_step, 2)
            act.activation(prob[:], score[:], ACT.Exp, bias=nmax).then_inc(exp_ready, 1)
            gu_hi_chunk(0, 0, 1)
            vo_half(1)
            gu_hi_chunk(0, 0, 2)
            gu_hi_chunk(0, 0, 3)
            down_hi(0, 0)
            act.wait_ge(h2_ready, 1)
            act.activation(h2_hi, h2[:], ACT.Copy).then_inc(h2_hi_ready, 1)
            act.wait_ge(x2_turned, 1)
            act.activation(x2T_hi[:, :, :], ps_t[:, 0].rearrange("p (c v) -> p c v", v=P),
                           ACT.Copy).then_inc(x2T_hi_ready, 1)
            for c in range(DC):
                gu_hi_chunk(0, 1, c)
            act.wait_ge(router_step, 2)
            act.activation(expd[:, 0:EXPERTS], logits[:, 0:EXPERTS], ACT.Exp, bias=lmax,
                           accum_out=lsum).then_inc(lexp_ready, 1)
            act.wait_ge(lexp_ready, 1)
            act.activation(spare[:, 0:1], lsum, ACT.Silu).then_inc(silu_table, 1)

            def pair_steps(pair):
                for s in range(SPP):
                    first = isinstance(pair, int) and pair == 0
                    if first and s < 2:
                        continue
                    silu_of(*before(pair, s, 2))
                    if is_last(pair, s):
                        down_hi(*before(pair, s, 1))
                        interT_hi_of(*before(pair, s, 2))
                        gu_hi_chunk(pair, s, 0)
                        gu_hi_chunk(pair, s, 1)
                        silu_of(*before(pair, s, 1))
                        gu_hi_chunk(pair, s, 2)
                        gu_hi_chunk(pair, s, 3)
                        continue
                    down_early = isinstance(pair, int) and s == 2
                    if down_early and not first:
                        down_hi(pair, 1)
                    gu_hi_chunk(pair, s, 0)
                    if down_early and first:
                        down_hi(pair, 1)
                    interT_hi_of(*before(pair, s, 2))
                    for c in range(1, DC):
                        gu_hi_chunk(pair, s, c)
                    if not down_early:
                        down_hi(*before(pair, s, 1))

            act.wait_ge(routed, 2)
            peel_both(act, pair_steps)
            last = SPP - 1
            interT_hi_of(PAIRS - 1, last - 1)
            last_down_hi(0)
            silu_of(PAIRS - 1, last)
            last_down_hi(1)
            last_down_hi(2)
            interT_hi_of(PAIRS - 1, last)
            act.wait_ge(half_summed, 1)
            act.activation(row_hi[:, half_cols[0]], ps_acc[:, half_cols[0]], ACT.Copy).then_inc(row_hi_ready, 1)
            for i in range(0, len(GATHERS), 2):
                copy_out(act, i, even_out)
                if i == 6:
                    act.wait_ge(right_joined, 2)
                    act.activation(row_hi[:, half_cols[1]], right, ACT.Copy).then_inc(row_hi_ready, 1)

        @block.vector
        def _(dve):
            def gu_lo_chunk(pair, s, c):
                buf = s % 2
                if c == 0:
                    dve.wait_ge(gu_in[s], (pair + 1) * 16)
                    buffer_free(dve, gu_summed, pair, s, qkv_done, s + 1)
                pair_wait(dve, gu_hi_done, pair, SPP * DC, s * DC + c + 1)
                dve.tensor_tensor(gu_lo[:, buf, c, :, 0:HALF], gu_chunk(s, c),
                                  gu_hi[:, buf, c, :, 0:HALF].bitcast(F32), ALU.subtract).then_inc(gu_lo_done, 1)

            def inter_of(pair, s):
                if isinstance(pair, int):
                    e = pair * 2 + s // HALVES
                    weight = comb[:, e:e + 1]
                else:
                    weight = comb[:, bass.ds(pair * 2 + s // HALVES, 1)]
                pair_wait(dve, silu_done, pair, SPP, s + 1)
                if is_last(pair, s):
                    dve.wait_ge(gu_summed, STEPS)
                pair_wait(dve, turned, pair, SPP, s - 2)
                dve.scalar_tensor_tensor(out=inter[:, s * HALF:(s + 1) * HALF], in0=silu[:, s % 2], scalar=weight,
                                         in1=ps_gu[:, 2 * (s % 2) + 1, 0:HALF], op0=ALU.mult,
                                         op1=ALU.mult).then_inc(inter_done, 1)

            def interT_lo_of(pair, s):
                a, b = GROUP[s]
                pair_wait(dve, turned_hi, pair, SPP, s + 1)
                if is_last(pair, s):
                    hi, lo = last_interT_hi[:, 0:b - a, :], last_interT_lo[:, 0:b - a, :]
                else:
                    pair_wait(dve, down_summed, pair, SPP, s - 1)
                    hi, lo = (t[:, s % 2, 0:b - a, :] for t in (interT_hi, interT_lo))
                dve.tensor_tensor(lo, ps_t[:, s % 2, 0:(b - a) * P].rearrange("p (c v) -> p c v", v=P),
                                  hi.bitcast(F32), ALU.subtract).then_inc(turned_lo, 1)

            dve.memset(zeros[:], 0.0).then_inc(zeros_ready, 1)
            dve.memset(ids_b[:], 0.0).then_inc(zeros_ready, 1)
            dve.wait_ge(ids_in, 16)
            dve.tensor_scalar(ids_f[:, 0], ids_sb[:], 0.0, float(P), ALU.is_lt, ALU.mult).then_inc(ids_fixed, 1)
            dve.wait_ge(ids_fixed, 1)
            dve.tensor_tensor(ids_f[:, 1], ids_f[:, 0], ids_sb[:], ALU.add).then_inc(ids_fixed, 1)
            dve.wait_ge(ids_fixed, 2)
            dve.wait_ge(zeros_ready, 2)
            dve.tensor_scalar(ids_b[0:TB, :], ids_f[:, 1], 0.0, float(P - 1), ALU.max, ALU.min).then_inc(ids_fixed, 1)
            dve.wait_ge(embT_in, 16)
            dve.wait_ge(cols_in, 16)
            dve.tensor_tensor(embT_w, embT_sb, cols_sb[:, NW:NW + DC, None].to_broadcast([P, DC, P]),
                              ALU.mult).then_inc(embT_scaled, 1)
            dve.wait_ge(consts, 4)
            for b in range(DC):
                dve.wait_ge(ids_spread, b + 1)
                dve.tensor_scalar(onehot[:, b * BANK:(b + 1) * BANK], ps_gu[:, b], row_index[:], 0.0,
                                  ALU.is_equal, ALU.add, accum_out=counts[:, b:b + 1]).then_inc(onehot_ready, 1)
            dve.wait_ge(projected, 1)
            dve.bn_stats(bn, ps_x[:]).then_inc(moments, 1)
            dve.wait_ge(moments, 1)
            dve.bn_aggr(mv, bn).then_inc(moments, 1)
            dve.wait_ge(moments, 2)
            dve.tensor_scalar(x1[:], ps_x[:], mean, None, ALU.subtract).then_inc(x1_ready, 1)
            dve.wait_ge(sumsq_done, 1)
            dve.tensor_scalar(c0, ps_t[:, 1, P:P + 1], RMS_EPS / D, RMS_EPS * RMS_EPS, ALU.mult,
                              ALU.add).then_inc(c0_ready, 1)
            dve.wait_ge(onehot_ready, 4)
            dve.tensor_reduce(count[:], counts[:], AX.X, ALU.add).then_inc(counted, 1)
            dve.wait_ge(counted, 1)
            dve.tensor_copy(count_wide[:], count[:, 0:1].to_broadcast([P, P])).then_inc(count_widened, 1)

            def qkv_lo(part, landed, chunks):
                dve.wait_ge(landed, 16)
                for c in chunks:
                    dve.wait_ge(wqkv_hi_done, part * DC + c + 1)
                    dve.tensor_tensor(wqkv_lo[part][:, c], (wv, wq, wk)[part][:, c],
                                      wqkv_hi[part][:, c].bitcast(F32), ALU.subtract).then_inc(wqkv_lo_done, 1)

            def add_bias(part, src, turned_part, ready):
                dve.wait_ge(turned_part, 1)
                bias = cols_sb[:, BQKV + part * DC:BQKV + (part + 1) * DC, None].to_broadcast([P, DC, P])
                dve.tensor_tensor(qkvT[:, part], src.rearrange("p (c v) -> p c v", v=P), bias,
                                  ALU.add).then_inc(ready, 1)

            qkv_lo(0, wv_in, range(2))
            dve.wait_ge(x1T_hi_ready, 1)
            dve.tensor_tensor(x1T_lo[:, :, :], ps_t[:, 0].rearrange("p (c v) -> p c v", v=P),
                              x1T_hi[:, :, :].bitcast(F32), ALU.subtract).then_inc(x1T_lo_ready, 1)
            qkv_lo(0, wv_in, range(2, DC))
            dve.wait_ge(c0_ready, 1)
            dve.tensor_tensor(v0, var, c0, ALU.add).then_inc(scale_step, 1)
            dve.wait_ge(scale_step, 1)
            dve.tensor_scalar(u2[:, 0:1], mean, mean, v0, ALU.mult, ALU.add).then_inc(scale_step, 1)
            dve.wait_ge(scale_step, 2)
            dve.tensor_scalar(u2[:, 1:2], u2[:, 0:1], LN_EPS, var, ALU.mult, ALU.add).then_inc(scale_step, 1)
            qkv_lo(1, wq_in, range(DC))
            qkv_lo(2, wk_in, range(2))
            add_bias(0, ps_gu[:, 0], v_turned, v_ready)
            qkv_lo(2, wk_in, range(2, DC - 1))
            dve.wait_ge(count_spread, 1)
            dve.tensor_copy(count_row[:], ps_t[:, 1, 0:P]).then_inc(counts_ready, 1)
            dve.tensor_scalar(absent_row[:], ps_t[:, 1, 0:P], 0.0, ABSENT, ALU.is_equal,
                              ALU.mult).then_inc(counts_ready, 1)
            add_bias(1, ps_gu[:, 1], q_turned, q_ready)
            dve.wait_ge(gate_split, 1)
            dve.tensor_tensor(gu_lo[:, 0, :, 0, HALF:], gate_w, gu_hi[:, 0, :, 0, HALF:].bitcast(F32),
                              ALU.subtract).then_inc(gate_split, 1)
            add_bias(2, ps_gu[:, 2], k_turned, k_ready)
            dve.wait_ge(scored, 1)
            dve.wait_ge(counts_ready, 2)
            dve.scalar_tensor_tensor(out=score[:], in0=ps_t[:, 1, 0:P], scalar=SCALE, in1=absent_row[:],
                                     op0=ALU.mult, op1=ALU.add).then_inc(softmax_step, 1)
            dve.wait_ge(softmax_step, 1)
            dve.tensor_reduce(nmax, score[:], AX.X, ALU.max, negate=True).then_inc(softmax_step, 1)
            dve.wait_ge(exp_ready, 1)
            dve.scalar_tensor_tensor(out=score[:], in0=prob[:], scalar=1.0, in1=count_row[:], op0=ALU.mult,
                                     op1=ALU.mult, accum_out=rsum).then_inc(prob_ready, 1)
            dve.wait_ge(prob_ready, 1)
            dve.reciprocal(rinv, rsum).then_inc(softmax_step, 1)
            dve.wait_ge(prob_turned, 1)
            dve.tensor_copy(probT[:], ps_t[:, 0, 0:P]).then_inc(probT_ready, 1)
            dve.wait_ge(gu_lo_done, 1)
            gu_lo_chunk(0, 0, 1)
            dve.wait_ge(attended, 1)
            dve.wait_ge(softmax_step, 3)
            dve.wait_ge(hb_ready, 1)
            dve.scalar_tensor_tensor(out=h2[:], in0=ps_x[:], scalar=rinv, in1=hb[:], op0=ALU.mult,
                                     op1=ALU.add, accum_out=h2_sum).then_inc(h2_ready, 1)
            dve.wait_ge(h2_ready, 1)
            dve.tensor_scalar(x2[:], h2[:], float(D), h2_sum, ALU.mult, ALU.subtract).then_inc(x2_ready, 1)
            dve.bn_stats(bn2, h2[:]).then_inc(moments2, 1)
            dve.wait_ge(moments2, 1)
            dve.bn_aggr(mv2, bn2).then_inc(moments2, 1)
            gu_lo_chunk(0, 0, 2)
            dve.wait_ge(x2T_hi_ready, 1)
            dve.tensor_tensor(x2T_lo[:, :, :], ps_t[:, 0].rearrange("p (c v) -> p c v", v=P),
                              x2T_hi[:, :, :].bitcast(F32), ALU.subtract).then_inc(x2T_lo_ready, 1)
            gu_lo_chunk(0, 0, 3)
            gu_lo_chunk(0, 1, 0)
            dve.memset(routing, NO_EXPERT).then_inc(router_step, 1)
            dve.wait_ge(routed, 1)
            dve.wait_ge(k2_ready, 1)
            dve.scalar_tensor_tensor(out=logits[:, 0:EXPERTS], in0=ps_gu[:, 0, HALF:HALF + EXPERTS], scalar=k2,
                                     in1=rows_sb[:, GB:GB + EXPERTS], op0=ALU.mult, op1=ALU.add).then_inc(routed, 1)
            dve.wait_ge(routed, 2)
            dve.tensor_reduce(lmax, logits[:, 0:EXPERTS], AX.X, ALU.max, negate=True).then_inc(router_step, 1)
            gu_lo_chunk(0, 1, 1)
            dve.wait_ge(lexp_ready, 1)
            dve.reciprocal(linv, lsum).then_inc(router_step, 1)
            dve.wait_ge(router_step, 3)
            dve.scalar_tensor_tensor(out=routing[:, 0:EXPERTS], in0=expd[:, 0:EXPERTS], scalar=linv,
                                     in1=rows_sb[:, EB:EB + EXPERTS], op0=ALU.mult,
                                     op1=ALU.add).then_inc(router_step, 1)
            dve.wait_ge(router_step, 4)
            dve.max(top[:, 0:8], routing).then_inc(router_step, 1)
            dve.wait_ge(router_step, 5)
            dve.memset(top[:, 2:8], NO_EXPERT).then_inc(router_step, 1)
            dve.wait_ge(router_step, 6)
            dve.match_replace(marked, top[:, 0:8], routing, TAKEN).then_inc(router_step, 1)
            dve.wait_ge(router_step, 7)
            dve.scalar_tensor_tensor(out=expd[:, 0:EXPERTS], in0=marked[:, 0:EXPERTS], scalar=TAKEN / 2,
                                     in1=routing[:, 0:EXPERTS], op0=ALU.is_lt, op1=ALU.mult).then_inc(router_step, 1)
            dve.wait_ge(router_step, 8)
            dve.tensor_scalar(comb[:, 0:EXPERTS], expd[:, 0:EXPERTS], k2, None, ALU.mult).then_inc(router_step, 1)
            gu_lo_chunk(0, 1, 2)
            dve.wait_ge(pool_lo_done, 1)
            dve.memset(spare[:, 1:2], 0.0).then_inc(gu_lo_done, 1)
            dve.wait_ge(router_step, 9)

            def pair_steps(pair):
                for s in range(SPP):
                    first = isinstance(pair, int) and pair == 0
                    if first and s < 2:
                        continue
                    inter_of(*before(pair, s, 2))
                    if is_last(pair, s):
                        interT_lo_of(*before(pair, s, 2))
                        gu_lo_chunk(pair, s, 0)
                        gu_lo_chunk(pair, s, 1)
                        inter_of(*before(pair, s, 1))
                        gu_lo_chunk(pair, s, 2)
                        gu_lo_chunk(pair, s, 3)
                        continue
                    gu_lo_chunk(pair, s, 0)
                    interT_lo_of(*before(pair, s, 2))
                    for c in range(1, DC):
                        gu_lo_chunk(pair, s, c)

            def down_lo_chunk(c):
                dve.wait_ge(dn_hi_done, STEPS + c)
                dve.tensor_tensor(last_dn_lo[:, c, :], raw_dn[:, GROUP[last][0] + c, :],
                                  last_dn_hi[:, c, :].bitcast(F32),
                                  ALU.subtract).then_inc(last_lo_done, 1)

            peel_both(dve, pair_steps)
            last = SPP - 1
            interT_lo_of(PAIRS - 1, last - 1)
            down_lo_chunk(0)
            inter_of(PAIRS - 1, last)
            down_lo_chunk(1)
            down_lo_chunk(2)
            interT_lo_of(PAIRS - 1, last)
            dve.wait_ge(row_hi_ready, 1)
            dve.tensor_tensor(row_lo[:, half_cols[0]], ps_acc[:, half_cols[0]],
                              row_hi[:, half_cols[0]].bitcast(F32), ALU.subtract).then_inc(row_lo_ready, 1)
            for i in range(1, len(GATHERS), 2):
                copy_out(dve, i, odd_out)
                if i == 5:
                    dve.wait_ge(half_summed, 2)
                    dve.tensor_copy(right, ps_x[:, 0:HW]).then_inc(right_joined, 1)
                    dve.wait_ge(right_joined, 1)
                    dve.tensor_tensor(right, right, ps_acc[:, half_cols[1]], ALU.add).then_inc(right_joined, 1)
                if i == 7:
                    dve.wait_ge(row_hi_ready, 2)
                    dve.tensor_tensor(row_lo[:, half_cols[1]], right, row_hi[:, half_cols[1]].bitcast(F32),
                                      ALU.subtract).then_inc(row_lo_ready, 1)

        @block.tensor
        def _(pe):
            def turn(dst, src, done):
                for c in range(DC):
                    ins = pe.transpose(dst[:, c * P:(c + 1) * P], src[:, c * P:(c + 1) * P], ident[:])
                ins.then_inc(done, 1)

            def keep_busy(products, bank):
                for _ in range(products):
                    pe.matmul(bank[:, 0:BANK], zeros[:].to_broadcast([P, P]), zeros[:].to_broadcast([P, BANK]),
                              start=True, stop=True)

            pe.wait_ge(zeros_ready, 1)
            keep_busy(WARM_UP, ps_acc)
            pe.wait_ge(ids_fixed, 3)
            pe.wait_ge(consts, 1)
            for j in range(TB):
                ins = pe.matmul(ps_gu[:, j // 4, (j % 4) * P:(j % 4 + 1) * P],
                                ident_b[:, j:j + 1].to_broadcast([P, P]), ids_b[:], start=True, stop=True)
                if j % 4 == 3:
                    ins.then_inc(ids_spread, 1)
            pe.wait_ge(embT_scaled, 1)
            for c in range(DC):
                pe.wait_ge(proj_in[c], 16)
                ins = pe.matmul(ps_x[:], embT_w[:, c], proj_sb[:, c], start=(c == 0), stop=(c == DC - 1))
            ins.then_inc(projected, 1)
            pe.wait_ge(rows_in, 16)
            pe.wait_ge(consts, 5)
            pe.wait_ge(onehot_ready, 4)
            one_row = ones[0:1, :].to_broadcast([1, P])
            pe.matmul(ps_gu[:, 3, 0:2 * EXPERTS], one_row, row_sb[:, D:], start=True, stop=True)
            pe.matmul(ps_acc[:], one_row, row_sb[:, 0:D], start=True, stop=True).then_inc(rows_spread, 1)
            pe.wait_ge(embT_squared, 1)
            for c in range(DC):
                ins = pe.matmul(ps_t[:, 1, P:P + 1], embT_sq[:, c], ones[:], start=(c == 0), stop=(c == DC - 1))
            ins.then_inc(sumsq_done, 1)
            pe.wait_ge(x1_ready, 1)
            pe.wait_ge(consts, 2)
            turn(ps_t[:, 0], x1[:], x1_turned)
            pe.wait_ge(count_widened, 1)
            pe.matmul(ps_t[:, 1, 0:P], count_wide[:], ident[:], start=True, stop=True).then_inc(count_spread, 1)
            keep_busy(2, ps_gu[:, 0])
            pe.wait_ge(x1T_hi_ready, 1)

            def project(part, between=None):
                for n, (x, w) in enumerate(((x1T_hi, wqkv_hi), (x1T_lo, wqkv_hi), (x1T_hi, wqkv_lo))):
                    if n == 1:
                        pe.wait_ge(x1T_lo_ready, 1)
                    if n == 2 and between:
                        between()
                    for c in range(DC):
                        if n == 2 and part == 2 and c == DC - 1:
                            pe.wait_ge(wk_last_lo_done, 1)
                        else:
                            pe.wait_ge((wqkv_hi_done, wqkv_hi_done, wqkv_lo_done)[n], part * DC + c + 1)
                        ins = pe.matmul(ps_gu[:, part], x[:, c], w[part][:, c], start=(n == 0 and c == 0),
                                        stop=(n == 2 and c == DC - 1))
                ins.then_inc(qkv_done, 1)

            def turn_part(part, done):
                pe.wait_ge(qkv_ready, part + 1)
                turn(ps_gu[:, part], qkv[:, part], done)

            project(0)
            project(1, between=lambda: turn_part(0, v_turned))
            project(2, between=lambda: turn_part(1, q_turned))
            pe.wait_ge(wo_in, 16)
            pe.wait_ge(v_ready, 1)
            pe.wait_ge(rows_ready, 2)
            for n in range(2):
                for c in range(DC):
                    ins = pe.matmul(vo_bank[n], qkvT[:, 0, c], wo[:, c, n * D // 2:(n + 1) * D // 2],
                                    start=(c == 0), stop=(c == DC - 1))
                    if n == 0 and c == 1:
                        turn_part(2, k_turned)
                ins.then_inc(vo_done, 1)
                if n == 0:
                    pe.wait_ge(q_ready, 1)
                    pe.wait_ge(k_ready, 1)
                    pe.wait_ge(counts_ready, 2)
                    for c in range(DC):
                        ins = pe.matmul(ps_t[:, 1, 0:P], qkvT[:, 1, c], qkvT[:, 2, c],
                                        start=(c == 0), stop=(c == DC - 1))
                    ins.then_inc(scored, 1)
            pe.wait_ge(prob_ready, 1)
            pe.transpose(ps_t[:, 0, 0:P], score[:], ident[:]).then_inc(prob_turned, 1)
            pe.wait_ge(probT_ready, 1)
            pe.wait_ge(h_ready, 1)
            for n in range(2):
                pe.wait_ge(vo_ready, n + 1)
                ins = pe.matmul(ps_x[:, n * D // 2:(n + 1) * D // 2], probT[:], vo[:, n * D // 2:(n + 1) * D // 2],
                                start=True, stop=True)
            ins.then_inc(attended, 1)
            keep_busy(7, ps_acc)
            pe.wait_ge(x2_ready, 1)
            turn(ps_t[:, 0], x2, x2_turned)
            keep_busy(3, ps_acc)
            pe.wait_ge(ident_ready, 1)
            pe.wait_ge(h2_hi_ready, 1)
            pe.matmul(ps_acc[:], ident_r[:], h2_hi, start=True, stop=False)

            def gate_up_sum(pair, s, chunks):
                buf = s % 2
                if 0 in chunks:
                    pair_wait(pe, silu_done, pair, SPP, s - 1)
                    pair_wait(pe, inter_done, pair, SPP, s - 1)
                order = [(c, g) for c in chunks for g in range(2)]
                if is_last(pair, s):
                    order.sort(key=lambda cg: cg[1])
                for c, g in order:
                    pair_wait(pe, gu_hi_done, pair, SPP * DC, s * DC + c + 1)
                    pair_wait(pe, gu_lo_done, pair, SPP * DC, s * DC + c + 1)
                    for n, (x, w) in enumerate(((x2T_hi, gu_hi), (x2T_hi, gu_lo), (x2T_lo, gu_hi))):
                        ins = pe.matmul(ps_gu[:, 2 * buf + g, 0:HALF], x[:, c], w[:, buf, c, g, 0:HALF],
                                        start=(c == 0 and n == 0), stop=(c == DC - 1 and n == 2))
                    if is_last(pair, s) and (c, g) == (DC - 1, 0):
                        ins.then_inc(last_gate_summed, 1)
                if DC - 1 in chunks:
                    ins.then_inc(gu_summed, 1)

            def first_gate_up_sum():
                for g in range(2):
                    n_cols = HALF + EXPERTS * (g == 0)
                    for n, (x, w) in enumerate(((x2T_hi, gu_hi), (x2T_lo, gu_hi), (x2T_hi, gu_lo))):
                        if g == 0:
                            pe.wait_ge(gate_split, 1 + (n == 2))
                            pe.wait_ge((x2T_hi_ready, x2T_lo_ready, x2T_hi_ready)[n], 1)
                        for c in range(DC):
                            if g == 0 and n != 1:
                                pe.wait_ge((gu_hi_done, None, gu_lo_done)[n], c + 1)
                            ins = pe.matmul(ps_gu[:, g, 0:n_cols], x[:, c], w[:, 0, c, g, 0:n_cols],
                                            start=(c == 0 and n == 0), stop=(c == DC - 1 and n == 2))
                    ins.then_inc((routed, gu_summed)[g], 1)

            def turn_inter(pair, s):
                a, b = GROUP[s]
                pair_wait(pe, inter_done, pair, SPP, s + 1)
                pair_wait(pe, turned_lo, pair, SPP, s - 1)
                for c in range(a, b):
                    ins = pe.transpose(ps_t[:, s % 2, (c - a) * P:(c - a + 1) * P],
                                       inter[:, c * P:(c + 1) * P], ident[:])
                ins.then_inc(turned, 1)

            def down_products(bank, cols, s, last=False, start=False, stop=False, ready=None):
                a, b = GROUP[s]
                if last:
                    x_hi, x_lo, w_hi, w_lo = last_interT_hi, last_interT_lo, last_dn_hi, last_dn_lo
                    parts = ((x_hi, w_hi), (x_hi, w_lo), (x_lo, w_hi))
                else:
                    x_hi, x_lo, w_hi, w_lo = (t[:, s % 2] for t in (interT_hi, interT_lo, dn_hi, dn_lo))
                    parts = ((x_hi, w_hi), (x_lo, w_hi), (x_hi, w_lo))
                for n, (x, w) in enumerate(parts):
                    for c in range(b - a):
                        if ready:
                            ready(n, c)
                        ins = pe.matmul(bank, x[:, c], w[:, c, cols], start=(start and c == n == 0),
                                        stop=(stop and c == b - a - 1 and n == 2))
                return ins

            def down_sum(pair, s, turn_within=None):
                def ready(n, c):
                    if c == 0:
                        if n == 0:
                            pair_wait(pe, turned_hi, pair, SPP, s + 1)
                        pair_wait(pe, (dn_hi_done, turned_lo, dn_lo_done)[n], pair, SPP, s + 1)
                    if turn_within and (n, c) == (1, 2):
                        turn_inter(*turn_within)

                if isinstance(pair, int) and (pair, s) == (PAIRS - 1, SPP - 3):
                    down_products(ps_acc[:, half_cols[0]], half_cols[0], s, ready=ready)
                else:
                    down_products(ps_acc[:], slice(0, D), s, ready=ready).then_inc(down_summed, 1)

            def pair_steps(pair):
                for s in range(SPP):
                    first = isinstance(pair, int) and pair == 0
                    if first and s == 0:
                        first_gate_up_sum()
                        pe.wait_ge(h2_lo_ready, 1)
                        pe.matmul(ps_acc[:], ident_r[:], h2_lo, start=False, stop=False)
                        continue
                    half = DC - 1 if first and s == 1 else DC // 2
                    gate_up_sum(pair, s, range(half))
                    turn_inter(*before(pair, s, 1))
                    gate_up_sum(pair, s, range(half, DC))
                    down_sum(*before(pair, s, 1), turn_within=(pair, s) if is_last(pair, s) else None)

            peel_both(pe, pair_steps)

            def last_ready(n, c):
                if n == 0:
                    pe.wait_ge(turned_hi, STEPS)
                    pe.wait_ge(dn_hi_done, STEPS + c)
                if n == 1:
                    pe.wait_ge(last_lo_done, c + 1)
                if n == 2 and c == 0:
                    pe.wait_ge(turned_lo, STEPS)

            down_products(ps_acc[:, half_cols[0]], half_cols[0], SPP - 1, last=True, stop=True,
                          ready=last_ready).then_inc(half_summed, 1)
            down_products(ps_x[:, 0:HW], half_cols[1], SPP - 3, start=True)
            for i, (n, first, blocks) in enumerate(GATHERS):
                pe.wait_ge(row_hi_ready, n + 1)
                pe.wait_ge(row_lo_ready, n + 1)
                if i >= GATHER_BANKS:
                    pe.wait_ge(even_out if i % 2 == 0 else odd_out, (i - GATHER_BANKS) // 2 + 1)
                for k in range(blocks):
                    token = (first + k) * P
                    for part in (row_hi, row_lo):
                        ins = pe.matmul(gather_bank[i % GATHER_BANKS][:, k * HW:(k + 1) * HW], onehot[:, token:token + P],
                                        part[:, half_cols[n]], start=(part is row_hi), stop=(part is row_lo))
                ins.then_inc(gathered, 1)
                if i == GATHER_BANKS - 1:
                    down_products(ps_x[:, 0:HW], half_cols[1], SPP - 1, last=True,
                                  stop=True).then_inc(half_summed, 1)


def before(pair, s, n, steps=4):
    return (pair, s - n) if s >= n else (pair - 1, s - n + steps)


def kernel(**inputs):
    import numpy as np
    import concourse.bacc as bacc
    from concourse.bass_utils import run_bass_kernel_spmd

    a = {k: np.asarray(v) for k, v in inputs.items()}
    x, emb = a["x"], a["L0_tok_emb_table"]
    T, D = x.shape[1], emb.shape[1]
    DC, TB = D // P, T // P
    w_gu, w_dn = a["L0_ffn_w_gate_up"], a["L0_ffn_w_down"]
    E, I = w_gu.shape[0], w_dn.shape[2]
    H = 2
    half = I // H

    def chunked(m):
        return m.reshape(DC, P, m.shape[1]).transpose(1, 0, 2)

    wq, wk, wv = np.split(a["L0_attn_w_qkv"], 3)
    bq, bk, bv = np.split(a["L0_attn_b_qkv"], 3)

    def column(v):
        return v.reshape(-1, P).T

    data = {
        "ids": x.reshape(P, TB).T,
        "embT": chunked(emb.T),
        "cols": np.concatenate([column(a["L0_tok_norm_weight"]), column(bv), column(bq), column(bk),
                                chunked(a["L0_ffn_gate_w"].T).reshape(P, DC * E)], axis=1),
        "rows": np.concatenate([a["L0_attn_b_out"], a["L0_ffn_gate_b"], a["L0_ffn_expert_bias"]])[None, :],
        "projT": chunked(a["L0_tok_proj_weight"].T),
        "wqkvT": np.stack([chunked(w.T) for w in (wv, wq, wk)]),
        "woT": chunked(a["L0_attn_w_out"].T),
        "gate_up": w_gu.reshape(E, 2, H, half, DC, P).transpose(0, 2, 5, 4, 1, 3),
        "down": w_dn.transpose(0, 2, 1).reshape(E // 2, 2 * I // P, P, D).transpose(0, 2, 1, 3),
    }
    data = {k: np.ascontiguousarray(v) for k, v in data.items()}
    nc = bacc.Bacc("TRN2", target_bir_lowering=False, num_devices=1)
    aps = [nc.dram_tensor(k, v.shape, mybir.dt.from_np(v.dtype), kind="ExternalInput").ap() for k, v in data.items()]
    out = nc.dram_tensor("out", (T, D), F32, kind="ExternalOutput").ap()
    tower_program(nc, *aps, out)
    result = run_bass_kernel_spmd(nc, [data], core_ids=[0])
    return result.results[0]["out"].reshape(1, T, D)
```
